# Optimizing a Trainium2 kernel written in Bass

```python
import numpy as np
import jax
import jax.numpy as jnp

def _softmax(x, axis=-1):
    return jax.nn.softmax(x, axis=axis)

def _gelu(x):
    return jax.nn.gelu(x, approximate=True)

def _silu(x):
    return jax.nn.silu(x)

def _sigmoid(x):
    return jax.nn.sigmoid(x)

def _layernorm(x, axis=-1, eps=1e-05):
    m = jnp.mean(x, axis=axis, keepdims=True)
    v = jnp.var(x, axis=axis, keepdims=True)
    return (x - m) / jnp.sqrt(v + eps)

def _scatter_add(tgt, idx, src, axis=0):
    return tgt.at[idx].add(src)

def _segment_sum(src, seg, n):
    return jax.ops.segment_sum(src, seg, n)
kernel_name = 'mk_gnn_ffn_d1_gnn_r32_49109c'

def setup_inputs(seed: int=0):
    np.random.seed(seed)
    _w = jnp.asarray

    def _rec_inputs():
        import jax
        import jax.numpy as jnp
        _gk = jax.random.key(seed)
        x = -8.776e-05 + 1 * jax.random.normal(jax.random.fold_in(_gk, 1), (10000, 512), jnp.float32)
        src = jax.random.randint(jax.random.fold_in(_gk, 2), (10000,), 0, 10000, jnp.int32)
        dst = jnp.minimum((10000 * jax.random.uniform(jax.random.fold_in(_gk, 3), (10000,)) ** 2.0).astype(jnp.int32), 9999)
        _o = jnp.argsort(dst, stable=True)
        src = src[_o]
        dst = dst[_o]
        return (x, src, dst)
    x, src, dst = _rec_inputs()

    def _L0_gnn_setup():
        import jax, jax.numpy as jnp
        import numpy as np
        N_NODES = 10000
        IN_FEAT = 512
        OUT_FEAT = 512
        N_EDGES = 5000
        key = jax.random.key(seed)
        kx, kw, ks, kd = jax.random.split(key, 4)
        x = jax.random.normal(kx, (N_NODES, IN_FEAT), dtype=jnp.float32)
        fan_in, fan_out = (2 * IN_FEAT, OUT_FEAT)
        limit = float(np.sqrt(6.0 / (fan_in + fan_out)))
        w = jax.random.uniform(kw, (OUT_FEAT, 2 * IN_FEAT), dtype=jnp.float32, minval=-limit, maxval=limit)
        src = jax.random.randint(ks, (N_EDGES,), 0, N_NODES, dtype=jnp.int32)
        dst = jax.random.randint(kd, (N_EDGES,), 0, N_NODES, dtype=jnp.int32)
        edge_index = jnp.stack([src, dst], axis=0)
        return {'x': x, 'w': w, 'edge_index': edge_index}
    _L0_gnn_all = _L0_gnn_setup()
    _L0_gnn_in = {k: v for k, v in _L0_gnn_all.items() if k in ('w',)}
    del _L0_gnn_all

    def _L0_ffn_setup():
        import jax, jax.numpy as jnp
        import numpy as np
        B, T, D, F, E, K = (8, 1024, 512, 64, 8, 2)

        def _moe_forward(x, Wr, br, W1, b1, W2, b2):
            Bx, Tx, Dx = x.shape
            xf = x.reshape(-1, Dx)
            logits = xf @ Wr + br
            probs = jax.nn.softmax(logits, axis=-1)
            vals, idx = jax.lax.top_k(probs, K)
            cw = (jax.nn.one_hot(idx, E, dtype=x.dtype) * vals[..., None]).sum(axis=1)

            def body(acc, params):
                W1e, b1e, W2e, b2e, cwe = params
                h = jax.nn.relu(xf @ W1e + b1e)
                y = h @ W2e + b2e
                return (acc + cwe[:, None] * y, None)
            out, _ = jax.lax.scan(body, jnp.zeros_like(xf), (W1, b1, W2, b2, cw.T))
            return out.reshape(Bx, Tx, Dx)
        key = jax.random.key(seed)
        k0, k1, k2, k3 = jax.random.split(key, 4)
        s_d = 1.0 / np.sqrt(D)
        s_f = 1.0 / np.sqrt(F)
        return {'x': jax.random.normal(k0, (B, T, D), jnp.float32), 'Wr': jax.random.uniform(k1, (D, E), jnp.float32, -s_d, s_d), 'br': jnp.zeros((E,), jnp.float32), 'W1': jax.random.uniform(k2, (E, D, F), jnp.float32, -s_d, s_d), 'b1': jnp.zeros((E, F), jnp.float32), 'W2': jax.random.uniform(k3, (E, F, D), jnp.float32, -s_f, s_f), 'b2': jnp.zeros((E, D), jnp.float32)}
    _L0_ffn_all = _L0_ffn_setup()
    _L0_ffn_in = {k: v for k, v in _L0_ffn_all.items() if k in ('Wr', 'br', 'W1', 'b1', 'W2', 'b2')}
    del _L0_ffn_all
    return {'x': x, 'src': src, 'dst': dst, 'L0_gnn_w': _L0_gnn_in['w'], 'L0_ffn_Wr': _L0_ffn_in['Wr'], 'L0_ffn_br': _L0_ffn_in['br'], 'L0_ffn_W1': _L0_ffn_in['W1'], 'L0_ffn_b1': _L0_ffn_in['b1'], 'L0_ffn_W2': _L0_ffn_in['W2'], 'L0_ffn_b2': _L0_ffn_in['b2']}

def reference(x, src, dst, L0_gnn_w, L0_ffn_Wr, L0_ffn_br, L0_ffn_W1, L0_ffn_b1, L0_ffn_W2, L0_ffn_b2):
    import jax
    import jax.numpy as jnp

    def _L0_gnn_ref(x, w, edge_index):
        import jax, jax.numpy as jnp
        import numpy as np
        N_NODES = 10000
        IN_FEAT = 512
        OUT_FEAT = 512
        N_EDGES = 5000
        src, dst = (edge_index[0], edge_index[1])
        msgs = x[src]
        summed = jax.ops.segment_sum(msgs, dst, num_segments=x.shape[0])
        deg = jax.ops.segment_sum(jnp.ones_like(dst, dtype=x.dtype), dst, num_segments=x.shape[0])
        neighbor_mean = summed / jnp.maximum(deg, 1.0)[:, None]
        message = jnp.concatenate([x, neighbor_mean], axis=-1)
        weighted = jnp.einsum('of,nf->no', w, message)
        return jax.nn.relu(weighted)

    def _L0_ffn_ref(x, Wr, br, W1, b1, W2, b2):
        import jax, jax.numpy as jnp
        import numpy as np
        B, T, D, F, E, K = (8, 1024, 512, 64, 8, 2)

        def _moe_forward(x, Wr, br, W1, b1, W2, b2):
            Bx, Tx, Dx = x.shape
            xf = x.reshape(-1, Dx)
            logits = xf @ Wr + br
            probs = jax.nn.softmax(logits, axis=-1)
            vals, idx = jax.lax.top_k(probs, K)
            cw = (jax.nn.one_hot(idx, E, dtype=x.dtype) * vals[..., None]).sum(axis=1)

            def body(acc, params):
                W1e, b1e, W2e, b2e, cwe = params
                h = jax.nn.relu(xf @ W1e + b1e)
                y = h @ W2e + b2e
                return (acc + cwe[:, None] * y, None)
            out, _ = jax.lax.scan(body, jnp.zeros_like(xf), (W1, b1, W2, b2, cw.T))
            return out.reshape(Bx, Tx, Dx)
        return _moe_forward(x, Wr, br, W1, b1, W2, b2)
    edge_index = jnp.stack([src, dst])
    x = x + _L0_gnn_ref(_layernorm(x, axis=-1), L0_gnn_w, edge_index)
    x = x + _L0_ffn_ref(_layernorm(x, axis=-1)[None], L0_ffn_Wr, L0_ffn_br, L0_ffn_W1, L0_ffn_b1, L0_ffn_W2, L0_ffn_b2)[0]
    return x

_drawn_inputs = setup_inputs


def setup_inputs(seed=0):
    import zlib

    import numpy as np

    out = dict(_drawn_inputs(seed))
    spreads = {'L0_ffn_br': (0.0, 0.1), 'L0_ffn_b1': (0.0, 0.764), 'L0_ffn_b2': (0.0, 0.301)}
    factors = {}
    for name, (base, spread) in spreads.items():
        noise = np.random.default_rng([zlib.crc32(name.encode()), seed]).standard_normal(out[name].shape)
        drawn = base * np.exp(spread * noise) if base else spread * noise
        out[name] = jnp.asarray(drawn.astype(out[name].dtype))
    for name, factor in factors.items():
        out[name] = (out[name] * factor).astype(out[name].dtype)
    return out
```

```python
from contextlib import ExitStack

import concourse.bass as bass
from concourse import mybir

F32 = mybir.dt.float32
F32R = mybir.dt.float32r
F16 = mybir.dt.float16
I32 = mybir.dt.int32
ALU = mybir.AluOpType
ACT = mybir.ActivationFunctionType
AX = mybir.AxisListType

P = 128
ITEMS = 2
TRIP = ITEMS * P
EPS = 1e-5
MSG_SCALE = 2048.0
TIE = 1e-38
NORM_STEPS = 2
EDGE_STEPS = 13
NORM2_STEPS = 6
ROUTE_STEPS = 10


def tile_of(k, c):
    return 2 * k + c, c % 2, k + c // 2


def moe_gnn_kernel(nc, x, edges, dst, w_gnn, w_router, b_router, w1, b1, w2, b2, out):
    N, D = x.shape
    E = dst.shape[0]
    KC = D // P
    X = b_router.shape[0]
    F = w1.shape[1] // X
    H = X * F
    TILES = -(-N // P)
    TAIL = N - (TILES - 1) * P
    EC = -(-E // P)
    EP = E // EC
    ER = E - EP * EC
    ALL_TRIPS = -(-E // TRIP)
    E_PAD = E + TRIP
    SP_ = 99
    SC = (E - 1) // SP_
    assert SP_ * SC == E - 1 and D == 4 * P and H == D and X == 8
    assert 128 * TILES >= N and P == 1 << 7 and TRIP == 1 << 8

    edge_list = nc.dram_tensor("edge_list", (E_PAD, 2), I32, kind="Internal").ap()
    deg_rows = nc.dram_tensor("deg_rows", (TILES, P + 1), F32, kind="Internal").ap()

    ctx = ExitStack()
    with ctx:
        def sb(name, shape, dt=F32):
            return ctx.enter_context(nc.sbuf_tensor(name, shape, dt))

        def pb(name, dt=F32):
            return ctx.enter_context(nc.psum_tensor(name, [P, 512], dt))

        def sem(name):
            return ctx.enter_context(nc.semaphore(name))

        wg_stage = sb("wg_stage", [P, 2 * KC, D])
        w1_stage = sb("w1_stage", [P, KC, H])
        w2_stage = sb("w2_stage", [P, KC, D])
        wr_stage = sb("wr_stage", [P, KC, X])
        wg_hi = sb("wg_hi", [P, 2 * KC, D], F32R)
        wg_lo = sb("wg_lo", [P, 2 * KC, D], F32R)
        w1_hi = sb("w1_hi", [P, KC, H], F32R)
        w1_lo = sb("w1_lo", [P, KC, H], F32R)
        w2_hi = sb("w2_hi", [P, KC, D], F32R)
        w2_lo = sb("w2_lo", [P, KC, D], F32R)
        wr = sb("wr", [P, KC, 2 * X], F32R)
        br16 = sb("br16", [2 * X, 1])
        b2_stage = sb("b2_stage", [3 * X, D])
        b2_hi = sb("b2_hi", [3 * X, D])
        b2_lo = sb("b2_lo", [3 * X, D])
        b2_rows = sb("b2_rows", [3 * X, D], F32R)
        b1_stage = sb("b1_stage", [2, H])
        b1_hi = sb("b1_hi", [2, H])
        b1_lo = sb("b1_lo", [2, H])
        b1_rows = sb("b1_rows", [2, H], F32R)
        ones2 = sb("ones2", [2, P], F32R)
        is_lo = sb("is_lo", [3 * X, 2])
        is_hi = sb("is_hi", [3 * X, 2])
        ones = sb("ones", [P, P])
        ident = sb("ident", [P, P])
        iota_i = sb("iota_i", [P, P], I32)
        iota = sb("iota", [P, P])
        iota16 = sb("iota16", [P, P], F16)
        eps_col = sb("eps_col", [P, 1])
        tie_bar = sb("tie_bar", [P, X, X])
        dst_all = sb("dst_all", [P, EC], I32)
        hi_i = sb("hi_i", [P, EC], I32)
        lo_i = sb("lo_i", [P, EC], I32)
        dst_tile = sb("dst_tile", [P, EC], F16)
        dst_node = sb("dst_node", [P, EC], F16)
        in_tile = sb("in_tile", [P, EC, TILES], F16)
        in_node = sb("in_node", [P, EC, P], F16)
        pad_rows = sb("pad_rows", [P, (E_PAD - E) // P, 2], I32)
        deg_tab = sb("deg_tab", [TILES, P + 1])
        degree = sb("degree", [TILES, P])
        count = sb("count", [TILES, 1])
        base_i = sb("base_i", [TILES, 1], I32)
        before = sb("before", [TILES, 2 * TILES])
        dst_a = sb("dst_a", [SP_, SC], I32)
        dst_b = sb("dst_b", [SP_, SC], I32)
        falls = sb("falls", [SP_, SC])
        fall = sb("fall", [SP_, 1])
        unsorted = sb("unsorted", [1, 1])
        is_sorted = sb("is_sorted", [1, 1])
        span = sb("span", [1, 2, TILES])
        trips_i = sb("trips_i", [1, TILES], I32)
        trips_s = sb("trips_s", [1, TILES], I32)
        trips_f = sb("trips_f", [1, TILES])
        more = sb("more", [1, TILES])
        plan = sb("plan", [1, 2, TILES], I32)
        x_in = sb("x_in", [P, 2, D])
        rdeg = sb("rdeg", [P, 2, P + 1])
        stat = sb("stat", [P, 6])
        mv = sb("mv", [P, 1 + ITEMS, 2])
        ln_v = sb("ln_v", [P, 1 + ITEMS])
        guess = sb("guess", [P, 1 + ITEMS])
        newton = sb("newton", [P, 1 + ITEMS])
        rstd = sb("rstd", [P, 1 + ITEMS])
        xn = sb("xn", [P, D])
        xt_hi = sb("xt_hi", [P, KC, P], F32R)
        xt_lo = sb("xt_lo", [P, KC, P], F32R)
        mt_hi = sb("mt_hi", [P, KC, P], F32R)
        mt_lo = sb("mt_lo", [P, KC, P], F32R)
        x1 = sb("x1", [P, 2, D])
        stat2 = sb("stat2", [P, 6])
        mv2 = sb("mv2", [P, 2])
        ln_v2 = sb("ln_v2", [P, 1])
        guess2 = sb("guess2", [P, 1])
        newton2 = sb("newton2", [P, 1])
        rstd2 = sb("rstd2", [P, 1])
        xn2 = sb("xn2", [P, D])
        x2t_hi = sb("x2t_hi", [P, KC, P], F32R)
        x2t_lo = sb("x2t_lo", [P, KC, P], F32R)
        lgt = sb("lgt", [2 * X, P])
        lg = sb("lg", [P, X])
        neg_max = sb("neg_max", [P, 1])
        lg_diff = sb("lg_diff", [P, X, X])
        beats = sb("beats", [P, X, X])
        rank = sb("rank", [P, X])
        ex = sb("ex", [P, X])
        ex_sum = sb("ex_sum", [P, 1])
        r_sum = sb("r_sum", [P, 1])
        ex_top = sb("ex_top", [P, X])
        gate = sb("gate", [P, X])
        gate_parts = sb("gate_parts", [P, 3, X])
        gt_rows = sb("gt_rows", [3 * X, P], F32R)
        hid = sb("hid", [P, X, F])
        ht_hi = sb("ht_hi", [P, KC, P], F32R)
        ht_lo = sb("ht_lo", [P, KC, P], F32R)
        o_sb = sb("o_sb", [P, 2, D])
        edge = sb("edge", [P, 3, ITEMS, 2], I32)
        raw = in_node[:, :, :].rearrange("p c n -> p (c n)").bitcast(F32)[:, 0:3 * ITEMS * D].rearrange(
            "p (s a d) -> p s a d", s=3, a=ITEMS)
        rel = sb("rel", [P, ITEMS])
        onehot = sb("onehot", [P, ITEMS, P], F16)
        weighted = sb("weighted", [P, ITEMS, P])
        w_edge = sb("w_edge", [P, ITEMS])
        stat_e = sb("stat_e", [P, ITEMS, 6])
        scale_e = sb("scale_e", [P, ITEMS])
        msg = sb("msg", [P, ITEMS, D])
        msg_hi = sb("msg_hi", [P, ITEMS, D], F16)
        msg_lo = sb("msg_lo", [P, ITEMS, D], F16)

        z_ps = pb("z_ps")
        h_ps = pb("h_ps")
        y_ps = pb("y_ps")
        t2_ps = pb("t2_ps")
        t13_ps = pb("t13_ps")
        m_ps = pb("m_ps")
        r_ps = pb("r_ps")

        s_dst = sem("dst_loaded")
        s_pairs = sem("sort_pairs_loaded")
        s_wg = [sem(f"wg_loaded{p}") for p in range(2)]
        s_w1 = sem("w1_loaded")
        s_w2 = sem("w2_loaded")
        s_small = sem("small_loaded")
        s_const = sem("pool_consts")
        s_pre = sem("vector_setup")
        s_hist = sem("histogram_done")
        s_span = sem("span_summed")
        s_deg = sem("deg_rows_stored")
        s_list = sem("edge_list_stored")
        s_apart = sem("waits_apart")
        s_whi = sem("weights_hi")
        s_wlo = sem("weights_lo")
        s_x = [sem(f"x_loaded{p}") for p in range(2)]
        s_rdeg = [sem(f"rdeg_loaded{p}") for p in range(2)]
        s_edge = [sem(f"edges_loaded{p}") for p in range(3)]
        s_raw = [[sem(f"rows_gathered{p}{a}") for a in range(ITEMS)] for p in range(3)]
        s_norm = sem("norm_steps")
        s_xn = sem("xn_ready")
        s_xt = sem("x_transposed")
        s_xthi = sem("xt_hi_ready")
        s_xtlo = sem("xt_lo_ready")
        s_es = sem("edge_steps")
        s_ln = sem("variance_logs")
        s_guess = sem("rstd_guessed")
        s_msg = sem("messages_normed")
        s_mhi = sem("messages_hi")
        s_mlo = sem("messages_lo")
        s_sum = sem("trips_summed")
        s_mthi = sem("mean_hi_ready")
        s_mtlo = sem("mean_lo_ready")
        s_z = sem("gnn_done")
        s_x1 = sem("x1_ready")
        s_n2 = sem("norm2_steps")
        s_ln2 = sem("variance2_logs")
        s_guess2 = sem("rstd2_guessed")
        s_x2t = sem("x2_transposed")
        s_x2hi = sem("x2t_hi_ready")
        s_x2lo = sem("x2t_lo_ready")
        s_lgt = sem("logits_done")
        s_lgc = sem("logits_copied")
        s_lg = sem("logits_transposed")
        s_rt = sem("route_steps")
        s_exp = sem("exp_ready")
        s_gt = sem("gate_transposed")
        s_gtc = sem("gate_rows_ready")
        s_h = sem("hidden_done")
        s_hg = sem("hidden_gated")
        s_ht = sem("hidden_transposed")
        s_hthi = sem("ht_hi_ready")
        s_htlo = sem("ht_lo_ready")
        s_y = sem("ffn_done")
        s_out = sem("out_ready")
        s_st = [sem(f"out_stored{p}") for p in range(2)]

        block = ctx.enter_context(nc.Block())

        def f32(ap):
            return ap.bitcast(F32)

        def at_least(eng, s, value):
            if not isinstance(value, int) or value > 0:
                eng.wait_ge(s, value)

        def wait_apart(eng, *waits):
            for s, n in waits:
                at_least(eng, s, n)
            eng.sem_inc(s_apart, 1)

        def periods(eng, period):
            first, last = 4, TILES - 3
            for u in range(-1, first):
                period(0, u)
            with eng.Fori(0, (last - first) // 2) as k:
                period(k, first)
                period(k, first + 1)
            for u in range(last, TILES + 1):
                period(0, u)

        def known(k, c):
            looped = not isinstance(k, int)
            return (looped or c >= 1, looped or 0 <= c < TILES, looped or c + 1 < TILES, looped or c + 2 < TILES)

        def trips_to(eng, further, v):
            return 0 if isinstance(v, int) and v == 0 else eng.snap(further) + v

        def rows_of(k, c):
            return P if not isinstance(k, int) or c < TILES - 1 else TAIL

        @block.sync
        def _(sync):
            sync.wait_ge(s_const, 1)
            sync.dma_start(dst_all[0:EP, :], dst[0:EP * EC].rearrange("(p c) -> p c", c=EC)).then_inc(s_dst, 16)
            sync.dma_start(dst_a[:, :], dst[0:E - 1].rearrange("(p c) -> p c", c=SC)).then_inc(s_pairs, 16)
            sync.dma_start(dst_b[:, :], dst[1:E].rearrange("(p c) -> p c", c=SC)).then_inc(s_pairs, 16)
            sync.dma_start(edge_list[0:E, :].rearrange("(q r) c -> q (r c)", q=16),
                           edges.rearrange("(q r) c -> q (r c)", q=16)).then_inc(s_list, 16)
            sync.wait_ge(s_const, 3)
            sync.dma_start(edge_list[E:E_PAD, :].rearrange("(p r) c -> p r c", p=P),
                           pad_rows[:, :, :]).then_inc(s_list, 16)
            wg_v = w_gnn.rearrange("(c p) n -> p c n", p=P)
            sync.dma_start(wg_stage[:, 0:KC, :], wg_v[:, 0:KC, :]).then_inc(s_wg[0], 16)

            def load_x(k, c):
                t, slot, _ = tile_of(k, c)
                n = rows_of(k, c)
                sync.dma_start(x_in[0:n, slot, :], x[bass.ds(t * P, n), :]).then_inc(s_x[slot], 16)

            def load_edges(k, c):
                t, slot, _ = tile_of(k, c)
                start = sync.value_load(plan[0:1, 0, bass.ds(t, 1)], min_val=0, max_val=E)
                sync.dma_start(edge[:, slot, :, :],
                               edge_list[bass.ds(start, TRIP), :].rearrange("(a p) c -> p a c", a=ITEMS)
                               ).then_inc(s_edge[slot], 16)
                sync.dma_start(rdeg[:, slot, :], deg_rows[bass.ds(t, 1), :].broadcast_to((P, P + 1))
                               ).then_inc(s_rdeg[slot], 16)

            load_x(0, 0)
            load_x(0, 1)
            sync.dma_start(wg_stage[:, KC:2 * KC, :], wg_v[:, KC:2 * KC, :]).then_inc(s_wg[1], 16)
            sync.wait_ge(s_pre, 24)
            sync.dma_start(deg_rows[:, :], deg_tab[:, :]).then_inc(s_deg, 16)
            sync.wait_ge(s_deg, 16)
            sync.wait_ge(s_list, 32)
            load_edges(0, 0)

            def period(k, c):
                prev, cur, nxt, pre = known(k, c)
                if pre:
                    if c >= 0:
                        sync.wait_ge(s_mtlo, tile_of(k, c)[0] + 1)
                    load_edges(k, c + 2)
                    if c >= 0:
                        sync.wait_ge(s_x1, tile_of(k, c)[0] + 1)
                        load_x(k, c + 2)
                if prev:
                    t, slot, _ = tile_of(k, c - 1)
                    n = rows_of(k, c - 1)
                    sync.wait_ge(s_out, t + 1)
                    sync.dma_start(out[bass.ds(t * P, n), :], o_sb[0:n, slot, :]).then_inc(s_st[slot], 16)

            periods(sync, period)
            sync.wait_ge(s_st[0], 16 * ((TILES + 1) // 2))
            sync.wait_ge(s_st[1], 16 * (TILES // 2))

        @block.gpsimd
        def _(pool):
            pool.memset(dst_all[:, :], -1).then_inc(s_const, 1)
            pool.memset(pad_rows[:, :, 0:1], 0).then_inc(s_const, 1)
            pool.memset(pad_rows[:, :, 1:2], -1).then_inc(s_const, 1)
            pool.iota(iota_i[:, :], pattern=[[1, P]], base=0, channel_multiplier=0).then_inc(s_const, 1)
            pool.iota(base_i[:, :], pattern=[[0, 1]], base=0, channel_multiplier=P).then_inc(s_const, 1)
            pool.memset(ones[:, :], 1.0).then_inc(s_const, 1)
            pool.memset(br16[:, :], 0.0).then_inc(s_const, 1)
            pool.memset(eps_col[:, :], EPS).then_inc(s_const, 1)
            pool.wait_ge(s_const, 8)
            pool.affine_select(out=ident[:, :], in_=ones[:, :], compare_op=ALU.is_equal, fill=0.0,
                               base=0, pattern=[[-1, P]], channel_multiplier=1).then_inc(s_const, 1)
            pool.affine_select(out=before[:, 0:TILES], in_=ones[0:TILES, 0:TILES], compare_op=ALU.is_gt, fill=0.0,
                               base=0, pattern=[[1, TILES]], channel_multiplier=-1).then_inc(s_const, 1)
            pool.affine_select(out=before[:, TILES:2 * TILES], in_=ones[0:TILES, 0:TILES], compare_op=ALU.is_equal,
                               fill=0.0, base=0, pattern=[[1, TILES]], channel_multiplier=-1).then_inc(s_const, 1)
            pool.memset(tie_bar[:, :, :], TIE).then_inc(s_const, 1)
            pool.affine_select(out=is_lo[:, 0:1], in_=ones[0:3 * X, 0:1], compare_op=ALU.is_ge, fill=0.0,
                               base=-X, pattern=[[0, 1]], channel_multiplier=1).then_inc(s_const, 1)
            pool.affine_select(out=is_lo[:, 1:2], in_=ones[0:3 * X, 0:1], compare_op=ALU.is_ge, fill=0.0,
                               base=-1, pattern=[[0, 1]], channel_multiplier=1).then_inc(s_const, 1)
            pool.wait_ge(s_const, 14)
            pool.affine_select(out=tie_bar[:, :, :], in_=tie_bar[:, :, :], compare_op=ALU.is_ge, fill=0.0,
                               base=0, pattern=[[-1, X], [1, X]], channel_multiplier=0).then_inc(s_const, 1)
            pool.affine_select(out=is_lo[:, 0:1], in_=is_lo[:, 0:1], compare_op=ALU.is_ge, fill=0.0,
                               base=2 * X - 1, pattern=[[0, 1]], channel_multiplier=-1).then_inc(s_const, 1)
            pool.wait_ge(s_const, 16)
            pool.tensor_scalar(is_hi[:, :], is_lo[:, :], -1.0, 1.0, op0=ALU.mult, op1=ALU.add).then_inc(s_const, 1)

            chunks = [(wg_lo, wg_hi, wg_stage, c) for c in range(2 * KC)]
            chunks += [(w1_lo, w1_hi, w1_stage, c) for c in range(KC)] + [(w2_lo, w2_hi, w2_stage, c) for c in range(KC)]
            for n, (lo, hi, stage, c) in enumerate(chunks):
                pool.wait_ge(s_whi, n + 1)
                pool.tensor_tensor(lo[:, c, :], stage[:, c, :], f32(hi[:, c, :]), op=ALU.subtract).then_inc(s_wlo, 1)

            def gather(slot, edges_there):
                wait_apart(pool, (s_edge[slot], edges_there))
                for a in range(ITEMS):
                    pool.indirect_dma_start(
                        out=raw[:, slot, a, :], out_offset=None, in_=x[:, :],
                        in_offset=bass.IndirectOffsetOnAxis(ap=edge[:, slot, a, 0:1], axis=0),
                        bounds_check=N - 1, oob_is_err=False).then_inc(s_raw[slot][a], 16)

            further = pool.alloc_register("pool_further")
            pool.reg_mov(further, 0)

            def messages(slot, trips):
                for a in range(ITEMS):
                    if a == 0:
                        wait_apart(pool, (s_es, trips * EDGE_STEPS + EDGE_STEPS), (s_mlo, trips))
                    pool.tensor_scalar(msg[:, a, :], raw[:, slot, a, :], mv[:, 1 + a, 0:1], scale_e[:, a:a + 1],
                                       op0=ALU.subtract, op1=ALU.mult).then_inc(s_msg, 1)
                pool.wait_ge(s_msg, trips * ITEMS + ITEMS)
                pool.wait_ge(s_mhi, trips + 1)
                at_least(pool, s_sum, trips)
                pool.tensor_tensor(msg_lo[:, :, :], msg[:, :, :], msg_hi[:, :, :], op=ALU.subtract).then_inc(s_mlo, 1)

            pool.wait_ge(s_pre, 24)
            gather(0, 16)

            def period(k, c):
                prev, cur, nxt, pre = known(k, c)
                if pre:
                    _, slot, uses = tile_of(k, c + 2)
                    gather(slot, 16 * (uses + 1))
                if nxt:
                    v, slot, _ = tile_of(k, c + 1)
                    trips_before = trips_to(pool, further, v)
                    wait_apart(pool, (s_es, trips_before * EDGE_STEPS + EDGE_STEPS - 1), (s_xt, v))
                    pool.tensor_scalar(xn[:, :], x_in[:, slot, :], mv[:, 0, 0:1], rstd[:, 0:1],
                                       op0=ALU.subtract, op1=ALU.mult).then_inc(s_xn, 1)
                    messages(slot, trips_before)
                    trips = pool.value_load(plan[0:1, 1, bass.ds(v, 1)], min_val=1, max_val=ALL_TRIPS)
                    with pool.If(trips > 1):
                        start = pool.value_load(plan[0:1, 0, bass.ds(v, 1)], min_val=0, max_val=E)
                        with pool.Fori(1, trips) as j:
                            done = pool.snap(further)
                            row = nc.s_assert_within(start + j * TRIP, min_val=0, max_val=E,
                                                     skip_runtime_bounds_check_because="a trip starts before the last edge")
                            row = pool.snap(row)
                            wait_apart(pool, (s_sum, done + v + 1))
                            pool.dma_start(edge[:, 2, :, :],
                                           edge_list[bass.ds(row, TRIP), :].rearrange("(a p) c -> p a c", a=ITEMS)
                                           ).then_inc(s_edge[2], 16)
                            gather(2, (done + 1) * 16)
                            messages(2, done + v + 1)
                            pool.reg_add(further, further, 1)

            periods(pool, period)

        @block.scalar
        def _(act):
            act.wait_ge(s_const, 1)
            act.dma_start(dst_all[EP:EP + 1, 0:ER], dst[EP * EC:E].rearrange("(p c) -> p c", p=1)).then_inc(s_dst, 16)
            act.dma_start(w1_stage[:, :, :], w1.rearrange("(c p) n -> p c n", p=P)).then_inc(s_w1, 16)
            act.dma_start(w2_stage[:, :, :], w2.rearrange("(c p) n -> p c n", p=P)).then_inc(s_w2, 16)
            act.dma_start(wr_stage[:, :, :], w_router.rearrange("(c p) n -> p c n", p=P)).then_inc(s_small, 16)
            act.wait_ge(s_const, 8)
            act.dma_start(br16[0:X, :], b_router.rearrange("(p c) -> p c", c=1)).then_inc(s_small, 16)
            for i in range(3):
                act.dma_start(b2_stage[i * X:(i + 1) * X, :], b2[:, :]).then_inc(s_small, 16)
            for i in range(2):
                act.dma_start(b1_stage[i:i + 1, :], b1.rearrange("(p c) -> p c", p=1)).then_inc(s_small, 16)
            chunks = [(wg_hi, wg_stage, c, s_wg[c // KC]) for c in range(2 * KC)]
            chunks += [(w1_hi, w1_stage, c, s_w1) for c in range(KC)] + [(w2_hi, w2_stage, c, s_w2) for c in range(KC)]
            for hi, stage, c, s in chunks:
                act.wait_ge(s, 16)
                act.activation(hi[:, c, :], stage[:, c, :], ACT.Copy).then_inc(s_whi, 1)

            further = act.alloc_register("act_further")
            act.reg_mov(further, 0)

            def guess_rstd(trips, lanes, norms):
                if lanes.start == 0:
                    act.wait_ge(s_norm, NORM_STEPS * norms)
                act.wait_ge(s_es, trips * EDGE_STEPS + 9)
                act.activation(ln_v[:, lanes], mv[:, lanes, 1], ACT.Ln, bias=eps_col[:, 0:1]).then_inc(s_ln, 1)
                act.wait_ge(s_ln, trips + 1)
                act.activation(guess[:, lanes], ln_v[:, lanes], ACT.Exp, scale=-0.5).then_inc(s_guess, 1)

            def message_hi(trips):
                act.wait_ge(s_msg, trips * ITEMS + ITEMS)
                at_least(act, s_sum, trips)
                act.activation(msg_hi[:, :, :], msg[:, :, :], ACT.Copy).then_inc(s_mhi, 1)

            def period(k, c):
                prev, cur, nxt, pre = known(k, c)
                u = tile_of(k, c)[0]
                if nxt:
                    trips = act.value_load(plan[0:1, 1, bass.ds(u + 1, 1)], min_val=1, max_val=ALL_TRIPS)
                if prev:
                    act.wait_ge(s_ht, u)
                    at_least(act, s_y, u - 1)
                    act.activation(ht_hi[:, :, :], t13_ps[:, :].rearrange("p (c n) -> p c n", c=KC), ACT.Copy).then_inc(s_hthi, 1)
                    act.wait_ge(s_gt, u)
                    act.activation(gt_rows[:, :], r_ps[0:3 * X, 256:256 + P], ACT.Copy).then_inc(s_gtc, 1)
                if nxt:
                    v = u + 1
                    trips_before = trips_to(act, further, v)
                    guess_rstd(trips_before, slice(0, 1 + ITEMS), v + 1)
                    message_hi(trips_before)
                if cur:
                    act.wait_ge(s_n2, NORM2_STEPS * u + 2)
                    act.activation(ln_v2[:, :], mv2[:, 1:2], ACT.Ln, bias=eps_col[:, 0:1]).then_inc(s_ln2, 1)
                    act.wait_ge(s_ln2, u + 1)
                    act.activation(guess2[:, :], ln_v2[:, :], ACT.Exp, scale=-0.5).then_inc(s_guess2, 1)
                if nxt:
                    with act.If(trips > 1):
                        with act.Fori(1, trips) as j:
                            guess_rstd(act.snap(further) + (v + 1), slice(1, 1 + ITEMS), None)
                            message_hi(act.snap(further) + (v + 1))
                            act.reg_add(further, further, 1)
                if cur:
                    act.wait_ge(s_x2t, u + 1)
                    at_least(act, s_h, u)
                    act.activation(x2t_hi[:, :, :], t2_ps[:, :].rearrange("p (c n) -> p c n", c=KC), ACT.Copy).then_inc(s_x2hi, 1)
                if nxt:
                    act.wait_ge(s_xt, v + 1)
                    at_least(act, s_z, v)
                    act.activation(xt_hi[:, :, :], t13_ps[:, :].rearrange("p (c n) -> p c n", c=KC), ACT.Copy).then_inc(s_xthi, 1)
                if cur:
                    act.wait_ge(s_lgt, u + 1)
                    act.activation(lgt[:, :], r_ps[0:2 * X, 0:P], ACT.Identity, bias=br16[:, 0:1]).then_inc(s_lgc, 1)
                if nxt:
                    act.wait_ge(s_sum, act.snap(further) + (v + 1))
                    act.activation(mt_hi[:, :, :], m_ps[:, :].rearrange("p (c n) -> p c n", c=KC), ACT.Copy,
                                   scale=1.0 / MSG_SCALE).then_inc(s_mthi, 1)
                if cur:
                    act.wait_ge(s_rt, ROUTE_STEPS * u + 2)
                    act.activation(ex[:, :], lg[:, :], ACT.Exp, bias=neg_max[:, 0:1],
                                   accum_out=ex_sum[:, 0:1]).then_inc(s_exp, 1)

            act.wait_ge(s_small, 16 * 7)
            act.preload_act_table_set("natural_log_exp_and_others")
            act.wait_ge(s_pre, 24)
            periods(act, period)

        @block.tensor
        def _(pe):
            pe.wait_ge(s_pre, 7)
            for c in range(EC):
                last = nc.tensor.matmul(r_ps[0:TILES, 0:P], in_tile[:, c, :], in_node[:, c, :],
                                        start=(c == 0), stop=(c == EC - 1))
            last.then_inc(s_hist, 1)
            pe.wait_ge(s_const, 11)
            pe.wait_ge(s_pre, 12)
            nc.tensor.matmul(m_ps[0:1, 0:2 * TILES], count[:, :], before[:, :], start=True, stop=True).then_inc(s_span, 1)
            nc.tensor.matmul(m_ps[0:1, 256:257], fall[:, :], ones[0:SP_, 0:1], start=True, stop=True).then_inc(s_span, 1)

            further = pe.alloc_register("pe_further")
            pe.reg_mov(further, 0)

            def product(bank, hi, lo, w_hi, w_lo, w_from, start, stop):
                for c in range(KC):
                    nc.tensor.matmul(bank[:, :], hi[:, c, :], w_hi[:, w_from + c, :], start=start and c == 0, stop=False)
                    nc.tensor.matmul(bank[:, :], hi[:, c, :], w_lo[:, w_from + c, :], start=False, stop=False)
                    last = nc.tensor.matmul(bank[:, :], lo[:, c, :], w_hi[:, w_from + c, :], start=False,
                                            stop=stop and c == KC - 1)
                return last

            def sum_messages(trips, fresh):
                pe.wait_ge(s_mlo, trips + 1)
                for a in range(ITEMS):
                    for c in range(KC):
                        for part in (msg_hi, msg_lo):
                            first = fresh and a == 0 and c == 0 and part is msg_hi
                            last = nc.tensor.matmul(m_ps[:, c * P:(c + 1) * P], part[:, a, c * P:(c + 1) * P],
                                                    onehot[:, a, :], start=first, stop=False, skip_group_check=True)
                last.then_inc(s_sum, 1)

            def transpose_rows(bank, rows):
                for c in range(KC):
                    last = nc.tensor.transpose(bank[:, c * P:(c + 1) * P], rows[:, c * P:(c + 1) * P], ident[:, :])
                return last

            def period(k, c):
                prev, cur, nxt, pre = known(k, c)
                u = tile_of(k, c)[0]
                v = u + 1
                if nxt:
                    trips = pe.value_load(plan[0:1, 1, bass.ds(v, 1)], min_val=1, max_val=ALL_TRIPS)
                if cur:
                    if isinstance(k, int) and c == 0:
                        pe.wait_ge(s_wlo, 2 * KC)
                    pe.wait_ge(s_xtlo, u + 1)
                    at_least(pe, s_x1, u)
                    product(z_ps, xt_hi, xt_lo, wg_hi, wg_lo, 0, True, False)
                if prev:
                    pe.wait_ge(s_hg, u)
                    transpose_rows(t13_ps, hid[:, :, :].rearrange("p x f -> p (x f)")).then_inc(s_ht, 1)
                    pe.wait_ge(s_rt, ROUTE_STEPS * u)
                    nc.tensor.transpose(r_ps[0:3 * X, 256:256 + P], gate_parts[:, :, :].rearrange("p a x -> p (a x)"),
                                        ident[:, :]).then_inc(s_gt, 1)
                if cur:
                    pe.wait_ge(s_mtlo, u + 1)
                    product(z_ps, mt_hi, mt_lo, wg_hi, wg_lo, KC, False, True).then_inc(s_z, 1)
                if prev:
                    pe.wait_ge(s_htlo, u)
                    at_least(pe, s_out, u - 1)
                    pe.wait_ge(s_gtc, u)
                    nc.tensor.matmul(y_ps[:, :], gt_rows[:, :], b2_rows[:, :], start=True, stop=False)
                    product(y_ps, ht_hi, ht_lo, w2_hi, w2_lo, 0, False, True).then_inc(s_y, 1)
                if cur:
                    pe.wait_ge(s_n2, NORM2_STEPS * u + NORM2_STEPS)
                    at_least(pe, s_x2lo, u)
                    transpose_rows(t2_ps, xn2[:, :]).then_inc(s_x2t, 1)
                if nxt:
                    pe.wait_ge(s_xn, v + 1)
                    at_least(pe, s_htlo, u)
                    transpose_rows(t13_ps, xn[:, :]).then_inc(s_xt, 1)
                    at_least(pe, s_mtlo, v)
                    sum_messages(trips_to(pe, further, v), True)
                    with pe.If(trips > 1):
                        with pe.Fori(1, trips) as j:
                            sum_messages(pe.snap(further) + (v + 1), False)
                            pe.reg_add(further, further, 1)
                if cur:
                    if isinstance(k, int) and c == 0:
                        pe.wait_ge(s_wlo, 4 * KC)
                        pe.wait_ge(s_pre, 35)
                    pe.wait_ge(s_x2lo, u + 1)
                    at_least(pe, s_gtc, u)
                    for part in (x2t_hi, x2t_lo):
                        for c_ in range(KC):
                            last = nc.tensor.matmul(r_ps[0:2 * X, 0:P], wr[:, c_, :], part[:, c_, :],
                                                    start=(part is x2t_hi and c_ == 0), stop=(part is x2t_lo and c_ == KC - 1))
                    last.then_inc(s_lgt, 1)
                    at_least(pe, s_hg, u)
                    nc.tensor.matmul(h_ps[:, :], ones2[:, :], b1_rows[:, :], start=True, stop=False)
                    for c_ in range(KC):
                        if c_ == KC - 1:
                            pe.wait_ge(s_lgc, u + 1)
                        nc.tensor.matmul(h_ps[:, :], x2t_hi[:, c_, :], w1_hi[:, c_, :], start=False, stop=False)
                    nc.tensor.transpose(r_ps[:, 128:128 + 2 * X], lgt[:, :], ident[0:2 * X, 0:2 * X]).then_inc(s_lg, 1)
                    for c_ in range(KC):
                        nc.tensor.matmul(h_ps[:, :], x2t_hi[:, c_, :], w1_lo[:, c_, :], start=False, stop=False)
                        last = nc.tensor.matmul(h_ps[:, :], x2t_lo[:, c_, :], w1_hi[:, c_, :], start=False, stop=(c_ == KC - 1))
                    last.then_inc(s_h, 1)

            pe.wait_ge(s_pre, 24)
            periods(pe, period)

        @block.vector
        def _(dve):
            def upto(n):
                dve.wait_ge(s_pre, n)

            dve.wait_ge(s_const, 17)
            dve.wait_ge(s_dst, 32)
            dve.tensor_scalar(hi_i[:, :], dst_all[:, :], 7, None, op0=ALU.arith_shift_right).then_inc(s_pre, 1)
            dve.tensor_scalar(lo_i[:, :], dst_all[:, :], P - 1, None, op0=ALU.bitwise_and).then_inc(s_pre, 1)
            dve.tensor_copy(iota16[:, :], iota_i[:, :]).then_inc(s_pre, 1)
            upto(1)
            dve.tensor_copy(dst_tile[:, :], hi_i[:, :]).then_inc(s_pre, 1)
            upto(2)
            dve.tensor_copy(dst_node[:, :], lo_i[:, :]).then_inc(s_pre, 1)
            upto(5)
            dve.tensor_tensor(in_tile[:, :, :], dst_tile[:, :].unsqueeze(2).broadcast_to((P, EC, TILES)),
                              iota16[:, 0:TILES].unsqueeze(1).broadcast_to((P, EC, TILES)), op=ALU.is_equal).then_inc(s_pre, 1)
            dve.tensor_tensor(in_node[:, :, :], dst_node[:, :].unsqueeze(2).broadcast_to((P, EC, P)),
                              iota16[:, :].unsqueeze(1).broadcast_to((P, EC, P)), op=ALU.is_equal).then_inc(s_pre, 1)
            dve.tensor_copy(iota[:, :], iota_i[:, :]).then_inc(s_pre, 1)
            dve.tensor_copy(deg_tab[:, P:P + 1], base_i[:, :]).then_inc(s_pre, 1)
            dve.wait_ge(s_pairs, 32)
            dve.tensor_tensor(falls[:, :], dst_a[:, :], dst_b[:, :], op=ALU.is_gt).then_inc(s_pre, 1)
            upto(10)
            dve.tensor_reduce(fall[:, :], falls[:, :], axis=AX.X, op=ALU.add).then_inc(s_pre, 1)
            dve.wait_ge(s_hist, 1)
            dve.tensor_reduce(count[:, :], r_ps[0:TILES, 0:P], axis=AX.X, op=ALU.add).then_inc(s_pre, 1)
            dve.tensor_scalar(degree[:, :], r_ps[0:TILES, 0:P], 1.0, None, op0=ALU.max).then_inc(s_pre, 1)
            upto(13)
            dve.reciprocal(deg_tab[:, 0:P], degree[:, :]).then_inc(s_pre, 1)
            dve.wait_ge(s_span, 2)
            dve.tensor_copy(span[:, :, :], m_ps[0:1, 0:2 * TILES].rearrange("p (a t) -> p a t", a=2)).then_inc(s_pre, 1)
            dve.tensor_scalar(unsorted[:, :], m_ps[0:1, 256:257], 1.0, None, op0=ALU.min).then_inc(s_pre, 1)
            upto(16)
            dve.tensor_scalar(is_sorted[:, :], unsorted[:, :], -1.0, 1.0, op0=ALU.mult, op1=ALU.add).then_inc(s_pre, 1)
            dve.tensor_scalar(trips_i[:, :], span[:, 1, :], float(TRIP - 1), None, op0=ALU.add).then_inc(s_pre, 1)
            upto(18)
            dve.tensor_scalar(trips_s[:, :], trips_i[:, :], 8, None, op0=ALU.arith_shift_right).then_inc(s_pre, 1)
            upto(19)
            dve.tensor_scalar(trips_f[:, :], trips_s[:, :], 1.0, None, op0=ALU.max).then_inc(s_pre, 1)
            upto(20)
            dve.tensor_scalar(more[:, :], trips_f[:, :], -1.0, float(ALL_TRIPS), op0=ALU.mult, op1=ALU.add).then_inc(s_pre, 1)
            upto(21)
            dve.scalar_tensor_tensor(more[:, :], more[:, :], unsorted[:, 0:1], trips_f[:, :],
                                     op0=ALU.mult, op1=ALU.add).then_inc(s_pre, 1)
            dve.tensor_scalar(plan[:, 0, :], span[:, 0, :], is_sorted[:, 0:1], None, op0=ALU.mult).then_inc(s_pre, 1)
            upto(22)
            dve.tensor_copy(plan[:, 1, :], more[:, :]).then_inc(s_pre, 1)
            dve.wait_ge(s_small, 16 * 7)
            dve.tensor_copy(b2_hi[:, :].bitcast(F32R), b2_stage[:, :]).then_inc(s_pre, 1)
            dve.tensor_copy(b1_hi[:, :].bitcast(F32R), b1_stage[:, :]).then_inc(s_pre, 1)
            dve.tensor_copy(wr[:, :, 0:X], wr_stage[:, :, :]).then_inc(s_pre, 1)
            upto(27)
            dve.tensor_tensor(b2_lo[:, :], b2_stage[:, :], b2_hi[:, :], op=ALU.subtract).then_inc(s_pre, 1)
            dve.tensor_tensor(b1_lo[:, :], b1_stage[:, :], b1_hi[:, :], op=ALU.subtract).then_inc(s_pre, 1)
            dve.tensor_tensor(wr[:, :, X:2 * X], wr_stage[:, :, :], f32(wr[:, :, 0:X]), op=ALU.subtract).then_inc(s_pre, 1)
            dve.tensor_scalar(b2_hi[:, :], b2_hi[:, :], is_hi[:, 0:1], None, op0=ALU.mult).then_inc(s_pre, 1)
            dve.tensor_scalar(b1_hi[:, :], b1_hi[:, :], is_hi[0:2, 1:2], None, op0=ALU.mult).then_inc(s_pre, 1)
            upto(32)
            dve.scalar_tensor_tensor(b2_rows[:, :], b2_lo[:, :], is_lo[:, 0:1], b2_hi[:, :], op0=ALU.mult, op1=ALU.add).then_inc(s_pre, 1)
            dve.scalar_tensor_tensor(b1_rows[:, :], b1_lo[:, :], is_lo[0:2, 1:2], b1_hi[:, :], op0=ALU.mult, op1=ALU.add).then_inc(s_pre, 1)
            dve.tensor_copy(ones2[:, :], ones[0:2, :]).then_inc(s_pre, 1)
            upto(35)

            further = dve.alloc_register("dve_further")
            dve.reg_mov(further, 0)

            def edge_part(slot, rd, trips, edges_there, lanes, between):
                base = trips * EDGE_STEPS

                def step(n):
                    dve.wait_ge(s_es, base + n)

                dve.wait_ge(s_edge[slot], edges_there)
                dve.tensor_scalar(rel[:, :], edge[:, slot, :, 1], rdeg[:, rd, P:P + 1], None,
                                  op0=ALU.subtract).then_inc(s_es, 1)
                between(0)
                step(1)
                at_least(dve, s_sum, trips)
                for a in range(ITEMS):
                    dve.tensor_scalar(onehot[:, a, :], iota[:, :], rel[:, a:a + 1], None, op0=ALU.is_equal).then_inc(s_es, 1)
                between(1)
                step(3)
                for a in range(ITEMS):
                    dve.scalar_tensor_tensor(weighted[:, a, :], onehot[:, a, :], 1.0, rdeg[:, rd, 0:P], op0=ALU.mult,
                                             op1=ALU.mult, accum_out=w_edge[:, a:a + 1]).then_inc(s_es, 1)
                for a in range(ITEMS):
                    dve.wait_ge(s_raw[slot][a], edges_there)
                    dve.bn_stats(stat_e[:, a, :], raw[:, slot, a, :]).then_inc(s_es, 1)
                between(2)
                for a in range(ITEMS):
                    wait_apart(dve, (s_es, base + 6 + a))
                    dve.bn_aggr(mv[:, 1 + a, :], stat_e[:, a, :]).then_inc(s_es, 1)
                between(3)
                dve.wait_ge(s_guess, trips + 1)
                dve.scalar_tensor_tensor(newton[:, lanes], guess[:, lanes], -0.5, guess[:, lanes],
                                         op0=ALU.mult, op1=ALU.mult).then_inc(s_es, 1)
                step(10)
                dve.scalar_tensor_tensor(newton[:, lanes], mv[:, lanes, 1], EPS, newton[:, lanes],
                                         op0=ALU.add, op1=ALU.mult).then_inc(s_es, 1)
                step(11)
                dve.scalar_tensor_tensor(rstd[:, lanes], newton[:, lanes], 1.5, guess[:, lanes],
                                         op0=ALU.add, op1=ALU.mult).then_inc(s_es, 1)
                step(12)
                dve.scalar_tensor_tensor(scale_e[:, :], rstd[:, 1:1 + ITEMS], MSG_SCALE, w_edge[:, :],
                                         op0=ALU.mult, op1=ALU.mult).then_inc(s_es, 1)

            def period(k, c):
                prev, cur, nxt, pre = known(k, c)
                u = tile_of(k, c)[0]
                slot_u = c % 2
                v, slot_v, uses_v = tile_of(k, c + 1)
                if prev:
                    dve.wait_ge(s_h, u)
                    at_least(dve, s_ht, u - 1)
                    dve.scalar_tensor_tensor(hid[:, :, :], h_ps[:, :].rearrange("p (x f) -> p x f", x=X), 0.0,
                                             gate[:, :].unsqueeze(2).broadcast_to((P, X, F)),
                                             op0=ALU.max, op1=ALU.mult).then_inc(s_hg, 1)
                if nxt:
                    dve.wait_ge(s_x[slot_v], 16 * (uses_v + 1))
                    at_least(dve, s_xn, v)
                    dve.bn_stats(stat[:, :], x_in[:, slot_v, :]).then_inc(s_norm, 1)
                    dve.wait_ge(s_rdeg[slot_v], 16 * (uses_v + 1))

                    def between(n):
                        if n == 0:
                            wait_apart(dve, (s_norm, NORM_STEPS * v + 1))
                            dve.bn_aggr(mv[:, 0, :], stat[:, :]).then_inc(s_norm, 1)
                        if n == 3:
                            dve.wait_ge(s_norm, NORM_STEPS * v + 2)
                        if n == 3 and prev:
                            dve.wait_ge(s_hthi, u)
                            at_least(dve, s_y, u - 1)
                            dve.tensor_tensor(ht_lo[:, :, :], t13_ps[:, :].rearrange("p (c n) -> p c n", c=KC),
                                              f32(ht_hi[:, :, :]), op=ALU.subtract).then_inc(s_htlo, 1)

                    trips_before = trips_to(dve, further, v)
                    at_least(dve, s_mlo, trips_before)
                    edge_part(slot_v, slot_v, trips_before, 16 * (uses_v + 1), slice(0, 1 + ITEMS), between)
                    trips = dve.value_load(plan[0:1, 1, bass.ds(v, 1)], min_val=1, max_val=ALL_TRIPS)
                elif prev:
                    dve.wait_ge(s_hthi, u)
                    at_least(dve, s_y, u - 1)
                    dve.tensor_tensor(ht_lo[:, :, :], t13_ps[:, :].rearrange("p (c n) -> p c n", c=KC),
                                      f32(ht_hi[:, :, :]), op=ALU.subtract).then_inc(s_htlo, 1)
                if cur:
                    dve.wait_ge(s_z, u + 1)
                    dve.scalar_tensor_tensor(x1[:, slot_u, :], z_ps[:, :], 0.0, x_in[:, slot_u, :],
                                             op0=ALU.max, op1=ALU.add).then_inc(s_x1, 1)
                    dve.wait_ge(s_x1, u + 1)
                    dve.bn_stats(stat2[:, :], x1[:, slot_u, :]).then_inc(s_n2, 1)
                    wait_apart(dve, (s_n2, NORM2_STEPS * u + 1))
                    dve.bn_aggr(mv2[:, :], stat2[:, :]).then_inc(s_n2, 1)
                    dve.wait_ge(s_n2, NORM2_STEPS * u + 2)
                    dve.wait_ge(s_guess2, u + 1)
                    dve.scalar_tensor_tensor(newton2[:, :], guess2[:, :], -0.5, guess2[:, :],
                                             op0=ALU.mult, op1=ALU.mult).then_inc(s_n2, 1)
                    dve.wait_ge(s_n2, NORM2_STEPS * u + 3)
                    dve.scalar_tensor_tensor(newton2[:, :], mv2[:, 1:2], EPS, newton2[:, :],
                                             op0=ALU.add, op1=ALU.mult).then_inc(s_n2, 1)
                    dve.wait_ge(s_n2, NORM2_STEPS * u + 4)
                    dve.scalar_tensor_tensor(rstd2[:, :], newton2[:, :], 1.5, guess2[:, :],
                                             op0=ALU.add, op1=ALU.mult).then_inc(s_n2, 1)
                    dve.wait_ge(s_n2, NORM2_STEPS * u + 5)
                    at_least(dve, s_x2t, u)
                    dve.tensor_scalar(xn2[:, :], x1[:, slot_u, :], mv2[:, 0:1], rstd2[:, 0:1],
                                      op0=ALU.subtract, op1=ALU.mult).then_inc(s_n2, 1)
                if prev:
                    dve.wait_ge(s_y, u)
                    _, slot, uses = tile_of(k, c - 1)
                    at_least(dve, s_st[slot], 16 * uses)
                    dve.tensor_tensor(o_sb[:, slot, :], y_ps[:, :], x1[:, slot, :], op=ALU.add).then_inc(s_out, 1)
                if nxt:
                    with dve.If(trips > 1):
                        with dve.Fori(1, trips) as j:
                            done = dve.snap(further)
                            dve.wait_ge(s_mlo, done + (v + 1))
                            edge_part(2, slot_v, done + (v + 1), (done + 1) * 16, slice(1, 1 + ITEMS), lambda n: None)
                            dve.reg_add(further, further, 1)
                if cur:
                    dve.wait_ge(s_x2hi, u + 1)
                    at_least(dve, s_h, u)
                    dve.tensor_tensor(x2t_lo[:, :, :], t2_ps[:, :].rearrange("p (c n) -> p c n", c=KC),
                                      f32(x2t_hi[:, :, :]), op=ALU.subtract).then_inc(s_x2lo, 1)
                if nxt:
                    dve.wait_ge(s_xthi, v + 1)
                    at_least(dve, s_z, v)
                    dve.tensor_tensor(xt_lo[:, :, :], t13_ps[:, :].rearrange("p (c n) -> p c n", c=KC),
                                      f32(xt_hi[:, :, :]), op=ALU.subtract).then_inc(s_xtlo, 1)
                if cur:
                    def routed(n):
                        dve.wait_ge(s_rt, ROUTE_STEPS * u + n)

                    dve.wait_ge(s_lg, u + 1)
                    at_least(dve, s_gt, u)
                    dve.tensor_reduce(lg[:, :], r_ps[:, 128:128 + 2 * X].rearrange("p (a x) -> p x a", a=2),
                                      axis=AX.X, op=ALU.add).then_inc(s_rt, 1)
                    routed(1)
                    dve.tensor_reduce(neg_max[:, :], lg[:, :], axis=AX.X, op=ALU.max, negate=True).then_inc(s_rt, 1)
                    dve.tensor_tensor(lg_diff[:, :, :], lg[:, :].unsqueeze(1).broadcast_to((P, X, X)),
                                      lg[:, :].unsqueeze(2).broadcast_to((P, X, X)), op=ALU.subtract).then_inc(s_rt, 1)
                    routed(3)
                    dve.tensor_tensor(beats[:, :, :], lg_diff[:, :, :], tie_bar[:, :, :], op=ALU.is_ge).then_inc(s_rt, 1)
                    routed(4)
                    dve.tensor_reduce(rank[:, :], beats[:, :, :], axis=AX.X, op=ALU.add).then_inc(s_rt, 1)
                if nxt:
                    dve.wait_ge(s_mthi, v + 1)
                    at_least(dve, s_z, v)
                    dve.scalar_tensor_tensor(mt_lo[:, :, :], m_ps[:, :].rearrange("p (c n) -> p c n", c=KC),
                                             1.0 / MSG_SCALE, f32(mt_hi[:, :, :]), op0=ALU.mult,
                                             op1=ALU.subtract).then_inc(s_mtlo, 1)
                if cur:
                    dve.wait_ge(s_exp, u + 1)
                    dve.reciprocal(r_sum[:, :], ex_sum[:, :]).then_inc(s_rt, 1)
                    routed(5)
                    dve.scalar_tensor_tensor(ex_top[:, :], rank[:, :], 1.5, ex[:, :], op0=ALU.is_lt, op1=ALU.mult).then_inc(s_rt, 1)
                    routed(7)
                    dve.tensor_scalar(gate[:, :], ex_top[:, :], r_sum[:, 0:1], None, op0=ALU.mult).then_inc(s_rt, 1)
                    dve.tensor_scalar(gate_parts[:, 0:2, :].bitcast(F32R), ex_top[:, :].unsqueeze(1).broadcast_to((P, 2, X)),
                                      r_sum[:, 0:1], None, op0=ALU.mult).then_inc(s_rt, 1)
                    routed(9)
                    dve.tensor_tensor(gate_parts[:, 2, :], gate[:, :], gate_parts[:, 0, :], op=ALU.subtract).then_inc(s_rt, 1)

            periods(dve, period)

    return nc


_OUT = ((10000, 512), "float32")


def kernel(x, src, dst, L0_gnn_w, L0_ffn_Wr, L0_ffn_br, L0_ffn_W1, L0_ffn_b1, L0_ffn_W2, L0_ffn_b2):
    import numpy as np
    import concourse.bacc as bacc
    from concourse.bass_utils import run_bass_kernel_spmd

    w1 = np.asarray(L0_ffn_W1)
    w2 = np.asarray(L0_ffn_W2)
    X, D, F = w1.shape
    arrays = {
        "x": np.asarray(x),
        "edges": np.stack([np.asarray(src), np.asarray(dst)], axis=1),
        "dst": np.asarray(dst),
        "w_gnn": np.asarray(L0_gnn_w).T,
        "w_router": np.asarray(L0_ffn_Wr),
        "b_router": np.asarray(L0_ffn_br),
        "w1": w1.transpose(1, 0, 2).reshape(D, X * F),
        "b1": np.asarray(L0_ffn_b1).reshape(X * F),
        "w2": w2.reshape(X * F, D),
        "b2": np.asarray(L0_ffn_b2),
    }
    nc = bacc.Bacc("TRN2", target_bir_lowering=False, num_devices=1)
    feed, args = {}, []
    for name, a in arrays.items():
        a = np.ascontiguousarray(a)
        feed[f"in_{name}"] = a
        args.append(nc.dram_tensor(f"in_{name}", a.shape, mybir.dt.from_np(a.dtype), kind="ExternalInput").ap())
    shape, dtype = _OUT
    args.append(nc.dram_tensor("out_0", shape, mybir.dt.from_np(np.dtype(dtype)), kind="ExternalOutput").ap())
    moe_gnn_kernel(nc, *args)
    r = run_bass_kernel_spmd(nc, [feed], core_ids=[0])
    return r.results[0]["out_0"]
```

```python
from contextlib import ExitStack

import concourse.bass as bass
from concourse import mybir
from concourse.bass import OrderedEngineSet

F32 = mybir.dt.float32
F32R = mybir.dt.float32r
F16 = mybir.dt.float16
I32 = mybir.dt.int32
ALU = mybir.AluOpType
ACT = mybir.ActivationFunctionType
AX = mybir.AxisListType

P = 128
ITEMS = 2
TRIP = ITEMS * P
UNROLL = 4
EPS = 1e-5
MSG_SCALE = 2048.0
TIE = 1e-38
NORM_STEPS = 2
EDGE_STEPS = 10
NORM2_STEPS = 6
ROUTE_STEPS = 10


def tile_of(k, c):
    return UNROLL * k + c


def uses(k, c, slots):
    return UNROLL // slots * k + c // slots


def moe_gnn_kernel(nc, x, edges, dst, w_gnn, w_router, b_router, w1, b1, w2, b2, out):
    N, D = x.shape
    E = dst.shape[0]
    KC = D // P
    X = b_router.shape[0]
    F = w1.shape[1] // X
    H = X * F
    TILES = -(-N // P)
    TAIL = N - (TILES - 1) * P
    EC = -(-E // P)
    EP = E // EC
    ER = E - EP * EC
    ALL_ITEMS = -(-E // P)
    E_PAD = E + TRIP
    SP_ = 99
    SC = (E - 1) // SP_
    assert SP_ * SC == E - 1 and D == 4 * P and H == D and X == 8
    assert P == 1 << 7

    edge_list = nc.dram_tensor("edge_list", (E_PAD, 2), I32, kind="Internal").ap()
    deg_rows = nc.dram_tensor("deg_rows", (TILES, P + 1), F32, kind="Internal").ap()

    ctx = ExitStack()
    with ctx:
        def sb(name, shape, dt=F32):
            return ctx.enter_context(nc.sbuf_tensor(name, shape, dt))

        def pb(name, dt=F32):
            return ctx.enter_context(nc.psum_tensor(name, [P, 512], dt))

        def sem(name):
            return ctx.enter_context(nc.semaphore(name))

        w_stage = sb("w_stage", [P, 2 * KC, D])
        wr_stage = sb("wr_stage", [P, KC, X])
        wg_hi = sb("wg_hi", [P, 2 * KC, D], F32R)
        wg_lo = sb("wg_lo", [P, 2 * KC, D], F32R)
        w1_hi = sb("w1_hi", [P, KC, H], F32R)
        w1_lo = sb("w1_lo", [P, KC, H], F32R)
        w2_hi = sb("w2_hi", [P, KC, D], F32R)
        w2_lo = sb("w2_lo", [P, KC, D], F32R)
        wr = sb("wr", [P, KC, 2 * X], F32R)
        br16 = sb("br16", [2 * X, 1])
        b2_stage = sb("b2_stage", [3 * X, D])
        b2_hi = sb("b2_hi", [3 * X, D])
        b2_lo = sb("b2_lo", [3 * X, D])
        b2_rows = sb("b2_rows", [3 * X, D], F32R)
        b1_stage = sb("b1_stage", [2, H])
        b1_hi = sb("b1_hi", [2, H])
        b1_lo = sb("b1_lo", [2, H])
        b1_rows = sb("b1_rows", [2, H], F32R)
        ones2 = sb("ones2", [2, P], F32R)
        is_lo = sb("is_lo", [3 * X, 2])
        is_hi = sb("is_hi", [3 * X, 2])
        ones = sb("ones", [P, P])
        ident = sb("ident", [P, P])
        iota_i = sb("iota_i", [P, P], I32)
        iota = sb("iota", [P, P])
        iota16 = sb("iota16", [P, P], F16)
        eps_col = sb("eps_col", [P, 1])
        tie_bar = sb("tie_bar", [P, X, X])
        dst_all = sb("dst_all", [P, EC], I32)
        hi_i = sb("hi_i", [P, EC], I32)
        lo_i = sb("lo_i", [P, EC], I32)
        dst_tile = sb("dst_tile", [P, EC], F16)
        dst_node = sb("dst_node", [P, EC], F16)
        in_tile = sb("in_tile", [P, EC, TILES], F16)
        in_node = sb("in_node", [P, EC, P], F16)
        pad_rows = sb("pad_rows", [P, (E_PAD - E) // P, 2], I32)
        deg_tab = sb("deg_tab", [TILES, P + 1])
        degree = sb("degree", [TILES, P])
        count = sb("count", [TILES, 1])
        base_i = sb("base_i", [TILES, 1], I32)
        before = sb("before", [TILES, 2 * TILES])
        dst_a = sb("dst_a", [SP_, SC], I32)
        dst_b = sb("dst_b", [SP_, SC], I32)
        falls = sb("falls", [SP_, SC])
        fall = sb("fall", [SP_, 1])
        unsorted = sb("unsorted", [1, 1])
        is_sorted = sb("is_sorted", [1, 1])
        span = sb("span", [1, 2, TILES])
        items_i = sb("items_i", [1, TILES], I32)
        items_s = sb("items_s", [1, TILES], I32)
        items_f = sb("items_f", [1, TILES])
        more = sb("more", [1, TILES])
        plan = sb("plan", [1, 2, TILES], I32)
        x_in = sb("x_in", [P, 4, D])
        rdeg = sb("rdeg", [P, 2, P + 1])
        stat = sb("stat", [P, 6])
        mv = sb("mv", [P, 2, 2])
        ln_v = sb("ln_v", [P, 2])
        guess = sb("guess", [P, 2])
        newton = sb("newton", [P, 2])
        rstd = sb("rstd", [P, 2])
        weight = sb("weight", [P, 2])
        scale = sb("scale", [P, 2])
        shift = sb("shift", [P, 2])
        xn = sb("xn", [P, D])
        xt_hi = sb("xt_hi", [P, KC, P], F32R)
        xt_lo = sb("xt_lo", [P, KC, P], F32R)
        mt_hi = sb("mt_hi", [P, 2, KC, P], F32R)
        mt_lo = sb("mt_lo", [P, 2, KC, P], F32R)
        x1 = sb("x1", [P, 2, D])
        stat2 = sb("stat2", [P, 6])
        mv2 = sb("mv2", [P, 2])
        ln_v2 = sb("ln_v2", [P, 1])
        guess2 = sb("guess2", [P, 1])
        newton2 = sb("newton2", [P, 1])
        rstd2 = sb("rstd2", [P, 1])
        shift2 = sb("shift2", [P, 1])
        xn2 = sb("xn2", [P, D])
        x2t_hi = sb("x2t_hi", [P, KC, P], F32R)
        x2t_lo = sb("x2t_lo", [P, KC, P], F32R)
        lgt = sb("lgt", [2 * X, P])
        lg = sb("lg", [P, X])
        neg_max = sb("neg_max", [P, 1])
        lg_diff = sb("lg_diff", [P, X, X])
        beats = sb("beats", [P, X, X])
        rank = sb("rank", [P, X])
        ex = sb("ex", [P, X])
        ex_sum = sb("ex_sum", [P, 1])
        r_sum = sb("r_sum", [P, 1])
        ex_top = sb("ex_top", [P, X])
        gate = sb("gate", [P, X])
        gate_parts = sb("gate_parts", [P, 3, X])
        gt_rows = sb("gt_rows", [3 * X, P], F32R)
        hid = sb("hid", [P, X, F])
        ht_hi = sb("ht_hi", [P, KC, P], F32R)
        ht_lo = sb("ht_lo", [P, KC, P], F32R)
        o_sb = sb("o_sb", [P, 2, D])
        edge = sb("edge", [P, 3, ITEMS, 2], I32)
        raw = in_node[:, :, :].rearrange("p c n -> p (c n)").bitcast(F32)[:, 0:3 * ITEMS * D].rearrange(
            "p (s a d) -> p s a d", s=3, a=ITEMS)
        rel = sb("rel", [P, 1])
        onehot = sb("onehot", [P, ITEMS, P], F16)
        weighted = sb("weighted", [P, P])
        stat_e = sb("stat_e", [P, 6])
        msg = sb("msg", [P, ITEMS, D])
        msg_hi = sb("msg_hi", [P, ITEMS, D], F16)
        msg_lo = sb("msg_lo", [P, ITEMS, D], F16)

        z_ps = [pb("z0_ps"), pb("z1_ps")]
        h_ps = pb("h_ps")
        y_ps = pb("y_ps")
        t2_ps = pb("t2_ps")
        t13_ps = pb("t13_ps")
        m_ps = pb("m_ps")
        r_ps = pb("r_ps")

        s_dst = sem("dst_loaded")
        s_pairs = sem("sort_pairs_loaded")
        s_wg = [sem(f"wg_loaded{p}") for p in range(2)]
        s_w1 = sem("w1_loaded")
        s_w2 = sem("w2_loaded")
        s_small = sem("small_loaded")
        s_const = sem("pool_consts")
        s_pre = sem("vector_setup")
        s_hist = sem("histogram_done")
        s_span = sem("span_summed")
        s_deg = sem("deg_rows_stored")
        s_list = sem("edge_list_stored")
        s_apart = sem("waits_apart")
        s_whi = sem("weights_hi")
        s_wlo = sem("weights_lo")
        s_x = [sem(f"x_loaded{p}") for p in range(4)]
        s_rdeg = [sem(f"rdeg_loaded{p}") for p in range(2)]
        s_edge = [sem(f"edges_loaded{p}") for p in range(3)]
        s_raw = [[sem(f"rows_gathered{p}{a}") for a in range(ITEMS)] for p in range(3)]
        s_norm = sem("norm_steps")
        s_xn = sem("xn_ready")
        s_xn2 = sem("xn2_ready")
        s_xt = sem("x_transposed")
        s_xthi = sem("xt_hi_ready")
        s_xtlo = sem("xt_lo_ready")
        s_es = sem("edge_steps")
        s_ln = sem("variance_logs")
        s_guess = sem("rstd_guessed")
        s_msg = sem("messages_normed")
        s_mhi = sem("messages_hi")
        s_mlo = sem("messages_lo")
        s_sum = sem("items_summed")
        s_mthi = sem("mean_hi_ready")
        s_mtlo = sem("mean_lo_ready")
        s_zx = sem("gnn_x_part_done")
        s_z = sem("gnn_done")
        s_x1 = sem("x1_ready")
        s_n2 = sem("norm2_steps")
        s_ln2 = sem("variance2_logs")
        s_guess2 = sem("rstd2_guessed")
        s_x2t = sem("x2_transposed")
        s_x2hi = sem("x2t_hi_ready")
        s_x2lo = sem("x2t_lo_ready")
        s_lgt = sem("logits_done")
        s_lgc = sem("logits_copied")
        s_lg = sem("logits_transposed")
        s_rt = sem("route_steps")
        s_exp = sem("exp_ready")
        s_gt = sem("gate_transposed")
        s_gtc = sem("gate_rows_ready")
        s_h = sem("hidden_done")
        s_hg = sem("hidden_gated")
        s_ht = sem("hidden_transposed")
        s_hthi = sem("ht_hi_ready")
        s_htlo = sem("ht_lo_ready")
        s_y = sem("ffn_done")
        s_out = sem("out_ready")
        s_st = [sem(f"out_stored{p}") for p in range(2)]

        block = ctx.enter_context(nc.Block())

        def f32(ap):
            return ap.bitcast(F32)

        def at_least(eng, s, value):
            if not isinstance(value, int) or value > 0:
                eng.wait_ge(s, value)

        def wait_apart(eng, *waits):
            for s, n in waits:
                at_least(eng, s, n)
            eng.sem_inc(s_apart, 1)

        def periods(eng, period):
            first, last = 3, 3 + (TILES - 4 - 3) // UNROLL * UNROLL
            for u in range(-3, first):
                period(0, u)
            with nc.Fori(0, (last - first) // UNROLL, engines=OrderedEngineSet([eng.engine]), hint_back_edge=True) as k:
                for i in range(UNROLL):
                    period(k, first + i)
            for u in range(last, TILES + 1):
                period(0, u)

        def known(k, c):
            looped = not isinstance(k, int)
            return [looped or 0 <= c + i < TILES for i in (-1, 0, 1, 2, 3)]

        def items_to(eng, further, v):
            return 0 if isinstance(v, int) and v == 0 else eng.snap(further) + v

        def buffer_free(n, a, first):
            return n if first else n - 1

        def more_items(eng, v, items, count, second, further, pairs, two_items):
            with eng.If(items > 1):
                second(1 if count == 0 else eng.snap(further) + (v + 1))
                eng.reg_add(further, further, 1)
                with eng.If(items > 2):
                    with eng.Fori(2, items, 2) as j:
                        two_items(j, eng.snap(further) + (v + 1), None if pairs is None else eng.snap(pairs))
                        eng.reg_add(further, further, 2)
                        if pairs is not None:
                            eng.reg_add(pairs, pairs, 1)

        def rows_of(k, c):
            return P if not isinstance(k, int) or c < TILES - 1 else TAIL

        @block.sync
        def _(sync):
            sync.wait_ge(s_const, 1)
            sync.dma_start(dst_all[0:EP, :], dst[0:EP * EC].rearrange("(p c) -> p c", c=EC)).then_inc(s_dst, 16)
            sync.dma_start(dst_a[:, :], dst[0:E - 1].rearrange("(p c) -> p c", c=SC)).then_inc(s_pairs, 16)
            sync.dma_start(dst_b[:, :], dst[1:E].rearrange("(p c) -> p c", c=SC)).then_inc(s_pairs, 16)
            sync.dma_start(edge_list[0:E, :].rearrange("(q r) c -> q (r c)", q=16),
                           edges.rearrange("(q r) c -> q (r c)", q=16)).then_inc(s_list, 16)
            sync.wait_ge(s_const, 3)
            sync.dma_start(edge_list[E:E_PAD, :].rearrange("(p r) c -> p r c", p=P),
                           pad_rows[:, :, :]).then_inc(s_list, 16)
            wg_v = w_gnn.rearrange("(c p) n -> p c n", p=P)
            sync.dma_start(w_stage[:, 0:KC, :], wg_v[:, 0:KC, :]).then_inc(s_wg[0], 16)

            def load_x(k, c):
                n = rows_of(k, c)
                sync.dma_start(x_in[0:n, c % 4, :], x[bass.ds(tile_of(k, c) * P, n), :]).then_inc(s_x[c % 4], 16)

            def load_edges(k, c):
                t, slot = tile_of(k, c), c % 2
                at_least(sync, s_raw[slot][1], 16 * uses(k, c, 2))
                start = sync.value_load(plan[0:1, 0, bass.ds(t, 1)], min_val=0, max_val=E)
                sync.dma_start(edge[:, slot, :, :],
                               edge_list[bass.ds(start, TRIP), :].rearrange("(a p) c -> p a c", a=ITEMS)
                               ).then_inc(s_edge[slot], 16)
                sync.dma_start(rdeg[:, slot, :], deg_rows[bass.ds(t, 1), :].broadcast_to((P, P + 1))
                               ).then_inc(s_rdeg[slot], 16)

            for t in range(4):
                load_x(0, t)
            sync.dma_start(w_stage[:, KC:2 * KC, :], wg_v[:, KC:2 * KC, :]).then_inc(s_wg[1], 16)
            sync.wait_ge(s_wlo, KC)
            sync.dma_start(w_stage[:, 0:KC, :], w1.rearrange("(c p) n -> p c n", p=P)).then_inc(s_w1, 16)
            sync.wait_ge(s_wlo, 2 * KC)
            sync.dma_start(w_stage[:, KC:2 * KC, :], w2.rearrange("(c p) n -> p c n", p=P)).then_inc(s_w2, 16)
            sync.wait_ge(s_pre, 24)
            sync.dma_start(deg_rows[:, :], deg_tab[:, :]).then_inc(s_deg, 16)
            sync.wait_ge(s_deg, 16)
            sync.wait_ge(s_list, 32)

            def period(k, c):
                prev, cur, nx1, nx2, nx3 = known(k, c)
                u = tile_of(k, c)
                if nx3:
                    if prev:
                        sync.wait_ge(s_lgt, u)
                    elif nx1:
                        sync.wait_ge(s_mtlo, u + 2)
                    load_edges(k, c + 3)
                    if prev:
                        load_x(k, c + 3)
                if prev:
                    n = rows_of(k, c - 1)
                    sync.wait_ge(s_out, u)
                    sync.dma_start(out[bass.ds((u - 1) * P, n), :], o_sb[0:n, (c - 1) % 2, :]).then_inc(s_st[(c - 1) % 2], 16)

            periods(sync, period)
            sync.wait_ge(s_st[0], 16 * ((TILES + 1) // 2))
            sync.wait_ge(s_st[1], 16 * (TILES // 2))

        @block.gpsimd
        def _(pool):
            pool.memset(dst_all[:, :], -1).then_inc(s_const, 1)
            pool.memset(pad_rows[:, :, 0:1], 0).then_inc(s_const, 1)
            pool.memset(pad_rows[:, :, 1:2], -1).then_inc(s_const, 1)
            pool.iota(iota_i[:, :], pattern=[[1, P]], base=0, channel_multiplier=0).then_inc(s_const, 1)
            pool.iota(base_i[:, :], pattern=[[0, 1]], base=0, channel_multiplier=P).then_inc(s_const, 1)
            pool.memset(ones[:, :], 1.0).then_inc(s_const, 1)
            pool.memset(br16[:, :], 0.0).then_inc(s_const, 1)
            pool.memset(eps_col[:, :], EPS).then_inc(s_const, 1)
            pool.wait_ge(s_const, 8)
            pool.affine_select(out=ident[:, :], in_=ones[:, :], compare_op=ALU.is_equal, fill=0.0,
                               base=0, pattern=[[-1, P]], channel_multiplier=1).then_inc(s_const, 1)
            pool.affine_select(out=before[:, 0:TILES], in_=ones[0:TILES, 0:TILES], compare_op=ALU.is_gt, fill=0.0,
                               base=0, pattern=[[1, TILES]], channel_multiplier=-1).then_inc(s_const, 1)
            pool.affine_select(out=before[:, TILES:2 * TILES], in_=ones[0:TILES, 0:TILES], compare_op=ALU.is_equal,
                               fill=0.0, base=0, pattern=[[1, TILES]], channel_multiplier=-1).then_inc(s_const, 1)
            pool.memset(tie_bar[:, :, :], TIE).then_inc(s_const, 1)
            pool.affine_select(out=is_lo[:, 0:1], in_=ones[0:3 * X, 0:1], compare_op=ALU.is_ge, fill=0.0,
                               base=-X, pattern=[[0, 1]], channel_multiplier=1).then_inc(s_const, 1)
            pool.affine_select(out=is_lo[:, 1:2], in_=ones[0:3 * X, 0:1], compare_op=ALU.is_ge, fill=0.0,
                               base=-1, pattern=[[0, 1]], channel_multiplier=1).then_inc(s_const, 1)
            pool.wait_ge(s_const, 14)
            pool.affine_select(out=tie_bar[:, :, :], in_=tie_bar[:, :, :], compare_op=ALU.is_ge, fill=0.0,
                               base=0, pattern=[[-1, X], [1, X]], channel_multiplier=0).then_inc(s_const, 1)
            pool.affine_select(out=is_lo[:, 0:1], in_=is_lo[:, 0:1], compare_op=ALU.is_ge, fill=0.0,
                               base=2 * X - 1, pattern=[[0, 1]], channel_multiplier=-1).then_inc(s_const, 1)
            pool.wait_ge(s_const, 16)
            pool.tensor_scalar(is_hi[:, :], is_lo[:, :], -1.0, 1.0, op0=ALU.mult, op1=ALU.add).then_inc(s_const, 1)

            chunks = [(wg_lo, wg_hi, c, c) for c in range(2 * KC)]
            chunks += [(w1_lo, w1_hi, c, c) for c in range(KC)] + [(w2_lo, w2_hi, c, KC + c) for c in range(KC)]
            for n, (lo, hi, c, at) in enumerate(chunks):
                pool.wait_ge(s_whi, n + 1)
                pool.tensor_tensor(lo[:, c, :], w_stage[:, at, :], f32(hi[:, c, :]), op=ALU.subtract).then_inc(s_wlo, 1)

            def gather(slot, edges_there):
                wait_apart(pool, (s_edge[slot], edges_there))
                for a in range(ITEMS):
                    pool.indirect_dma_start(
                        out=raw[:, slot, a, :], out_offset=None, in_=x[:, :],
                        in_offset=bass.IndirectOffsetOnAxis(ap=edge[:, slot, a, 0:1], axis=0),
                        bounds_check=N - 1, oob_is_err=False).then_inc(s_raw[slot][a], 16)

            further = pool.alloc_register("pool_further")
            pairs = pool.alloc_register("pool_pairs")
            pool.reg_mov(further, 0)
            pool.reg_mov(pairs, 0)

            def message_lo(n, a, first):
                pool.wait_ge(s_msg, n + 1)
                pool.wait_ge(s_mhi, n + 1)
                at_least(pool, s_sum, buffer_free(n, a, first))
                pool.tensor_tensor(msg_lo[:, a, :], msg[:, a, :], msg_hi[:, a, :], op=ALU.subtract).then_inc(s_mlo, 1)

            pool.wait_ge(s_pre, 24)

            def period(k, c):
                prev, cur, nx1, nx2, nx3 = known(k, c)
                if nx3:
                    gather((c + 3) % 2, 16 * (uses(k, c + 3, 2) + 1))
                if nx2:
                    v = tile_of(k, c + 2)
                    items = pool.value_load(plan[0:1, 1, bass.ds(v, 1)], min_val=1, max_val=ALL_ITEMS)
                    message_lo(items_to(pool, further, v), 0, True)

                    def two_items(j, n, turns):
                        start = pool.value_load(plan[0:1, 0, bass.ds(v, 1)], min_val=0, max_val=E)
                        row = pool.snap(nc.s_assert_within(start + j * P, min_val=0, max_val=E,
                                                           skip_runtime_bounds_check_because="a turn starts before the last edge"))
                        wait_apart(pool, (s_sum, n))
                        pool.dma_start(edge[:, 2, :, :],
                                       edge_list[bass.ds(row, TRIP), :].rearrange("(a p) c -> p a c", a=ITEMS)
                                       ).then_inc(s_edge[2], 16)
                        gather(2, (turns + 1) * 16)
                        for a in range(ITEMS):
                            message_lo(n + a, a, False)

                    more_items(pool, v, items, c + 2, lambda n: message_lo(n, 1, False), further, pairs, two_items)

            periods(pool, period)

        @block.scalar
        def _(act):
            act.wait_ge(s_const, 1)
            act.dma_start(dst_all[EP:EP + 1, 0:ER], dst[EP * EC:E].rearrange("(p c) -> p c", p=1)).then_inc(s_dst, 16)
            act.dma_start(wr_stage[:, :, :], w_router.rearrange("(c p) n -> p c n", p=P)).then_inc(s_small, 16)
            act.wait_ge(s_const, 8)
            act.dma_start(br16[0:X, :], b_router.rearrange("(p c) -> p c", c=1)).then_inc(s_small, 16)
            for i in range(3):
                act.dma_start(b2_stage[i * X:(i + 1) * X, :], b2[:, :]).then_inc(s_small, 16)
            for i in range(2):
                act.dma_start(b1_stage[i:i + 1, :], b1.rearrange("(p c) -> p c", p=1)).then_inc(s_small, 16)
            chunks = [(wg_hi, c, c, s_wg[c // KC]) for c in range(2 * KC)]
            chunks += [(w1_hi, c, c, s_w1) for c in range(KC)] + [(w2_hi, c, KC + c, s_w2) for c in range(KC)]
            for hi, c, at, s in chunks:
                act.wait_ge(s, 16)
                act.activation(hi[:, c, :], w_stage[:, at, :], ACT.Copy).then_inc(s_whi, 1)

            further = act.alloc_register("act_further")
            act.reg_mov(further, 0)

            def edge_rows(n, slot, a, first, tile=None):
                lanes = slice(1, 2) if tile is None else slice(0, 2)
                if tile is not None:
                    act.wait_ge(s_norm, NORM_STEPS * (tile[0] + 1))
                act.wait_ge(s_es, n * EDGE_STEPS + 5)
                act.activation(ln_v[:, lanes], mv[:, lanes, 1], ACT.Ln, bias=eps_col[:, 0:1]).then_inc(s_ln, 1)
                act.wait_ge(s_ln, n + 1)
                act.activation(guess[:, lanes], ln_v[:, lanes], ACT.Exp, scale=-0.5).then_inc(s_guess, 1)
                yield
                act.wait_ge(s_es, n * EDGE_STEPS + 10)
                if tile is not None:
                    at_least(act, s_xt, tile[0])
                    act.activation(xn[:, :], x_in[:, tile[1], :], ACT.Identity, bias=shift[:, 0:1],
                                   scale=scale[:, 0:1]).then_inc(s_xn, 1)
                at_least(act, s_mlo, buffer_free(n, a, first))
                act.activation(msg[:, a, :], raw[:, slot, a, :], ACT.Identity, bias=shift[:, 1:2],
                               scale=scale[:, 1:2]).then_inc(s_msg, 1)
                at_least(act, s_sum, buffer_free(n, a, first))
                act.activation(msg_hi[:, a, :], raw[:, slot, a, :], ACT.Identity, bias=shift[:, 1:2],
                               scale=scale[:, 1:2]).then_inc(s_mhi, 1)
                yield

            def item(n, slot, a):
                for _ in edge_rows(n, slot, a, False):
                    pass

            def two_items(j, n, turns):
                for a in range(ITEMS):
                    item(n + a, 2, a)

            def period(k, c):
                prev, cur, nx1, nx2, nx3 = known(k, c)
                u = tile_of(k, c)
                if nx2:
                    v = u + 2
                    items = act.value_load(plan[0:1, 1, bass.ds(v, 1)], min_val=1, max_val=ALL_ITEMS)
                if prev:
                    act.wait_ge(s_ht, u)
                    at_least(act, s_y, u - 1)
                    act.activation(ht_hi[:, :, :], t13_ps[:, :].rearrange("p (c n) -> p c n", c=KC), ACT.Copy).then_inc(s_hthi, 1)
                    act.wait_ge(s_gt, u)
                    act.activation(gt_rows[:, :], r_ps[0:3 * X, 256:256 + P], ACT.Copy).then_inc(s_gtc, 1)
                if nx2:
                    rows = edge_rows(items_to(act, further, v), c % 2, 0, True, (v, (c + 2) % 4))
                    next(rows)
                if cur:
                    act.wait_ge(s_n2, NORM2_STEPS * u + 2)
                    act.activation(ln_v2[:, :], mv2[:, 1:2], ACT.Ln, bias=eps_col[:, 0:1]).then_inc(s_ln2, 1)
                    act.wait_ge(s_ln2, u + 1)
                    act.activation(guess2[:, :], ln_v2[:, :], ACT.Exp, scale=-0.5).then_inc(s_guess2, 1)
                if nx2:
                    next(rows)
                if cur:
                    act.wait_ge(s_n2, NORM2_STEPS * u + 6)
                    at_least(act, s_x2t, u)
                    act.activation(xn2[:, :], x1[:, c % 2, :], ACT.Identity, bias=shift2[:, 0:1],
                                   scale=rstd2[:, 0:1]).then_inc(s_xn2, 1)
                if nx2:
                    more_items(act, v, items, c + 2, lambda n: item(n, c % 2, 1), further, None, two_items)
                if cur:
                    act.wait_ge(s_x2t, u + 1)
                    at_least(act, s_h, u)
                    act.activation(x2t_hi[:, :, :], t2_ps[:, :].rearrange("p (c n) -> p c n", c=KC), ACT.Copy).then_inc(s_x2hi, 1)
                if nx2:
                    act.wait_ge(s_xt, v + 1)
                    act.activation(xt_hi[:, :, :], t13_ps[:, :].rearrange("p (c n) -> p c n", c=KC), ACT.Copy).then_inc(s_xthi, 1)
                if cur:
                    act.wait_ge(s_lgt, u + 1)
                    act.activation(lgt[:, :], r_ps[0:2 * X, 0:P], ACT.Identity, bias=br16[:, 0:1]).then_inc(s_lgc, 1)
                if nx2:
                    act.wait_ge(s_sum, act.snap(further) + (v + 1))
                    at_least(act, s_z, u + 1)
                    act.activation(mt_hi[:, c % 2, :, :], m_ps[:, :].rearrange("p (c n) -> p c n", c=KC), ACT.Copy,
                                   scale=1.0 / MSG_SCALE).then_inc(s_mthi, 1)
                if cur:
                    act.wait_ge(s_rt, ROUTE_STEPS * u + 2)
                    act.activation(ex[:, :], lg[:, :], ACT.Exp, bias=neg_max[:, 0:1],
                                   accum_out=ex_sum[:, 0:1]).then_inc(s_exp, 1)

            act.wait_ge(s_small, 16 * 7)
            act.preload_act_table_set("natural_log_exp_and_others")
            act.wait_ge(s_pre, 24)
            periods(act, period)

        @block.tensor
        def _(pe):
            pe.wait_ge(s_pre, 7)
            for c in range(EC):
                last = nc.tensor.matmul(r_ps[0:TILES, 0:P], in_tile[:, c, :], in_node[:, c, :],
                                        start=(c == 0), stop=(c == EC - 1))
            last.then_inc(s_hist, 1)
            pe.wait_ge(s_const, 11)
            pe.wait_ge(s_pre, 12)
            nc.tensor.matmul(m_ps[0:1, 0:2 * TILES], count[:, :], before[:, :], start=True, stop=True).then_inc(s_span, 1)
            nc.tensor.matmul(m_ps[0:1, 256:257], fall[:, :], ones[0:SP_, 0:1], start=True, stop=True).then_inc(s_span, 1)

            further = pe.alloc_register("pe_further")
            pe.reg_mov(further, 0)

            def product(bank, hi, lo, w_hi, w_lo, w_from, start, stop):
                for c in range(KC):
                    nc.tensor.matmul(bank[:, :], hi[:, c, :], w_hi[:, w_from + c, :], start=start and c == 0, stop=False)
                    nc.tensor.matmul(bank[:, :], hi[:, c, :], w_lo[:, w_from + c, :], start=False, stop=False)
                    last = nc.tensor.matmul(bank[:, :], lo[:, c, :], w_hi[:, w_from + c, :], start=False,
                                            stop=stop and c == KC - 1)
                return last

            def sum_item(n, a, first):
                pe.wait_ge(s_mlo, n + 1)
                for c in range(KC):
                    for part in (msg_hi, msg_lo):
                        last = nc.tensor.matmul(m_ps[:, c * P:(c + 1) * P], part[:, a, c * P:(c + 1) * P],
                                                onehot[:, a, :], start=first and c == 0 and part is msg_hi,
                                                stop=False, skip_group_check=True)
                last.then_inc(s_sum, 1)

            def two_items(j, n, turns):
                for a in range(ITEMS):
                    sum_item(n + a, a, False)

            def transpose_rows(bank, rows):
                for c in range(KC):
                    last = nc.tensor.transpose(bank[:, c * P:(c + 1) * P], rows[:, c * P:(c + 1) * P], ident[:, :])
                return last

            def period(k, c):
                prev, cur, nx1, nx2, nx3 = known(k, c)
                u = tile_of(k, c)
                v = u + 2
                if nx2:
                    items = pe.value_load(plan[0:1, 1, bass.ds(v, 1)], min_val=1, max_val=ALL_ITEMS)
                if cur:
                    if isinstance(k, int) and c == 0:
                        pe.wait_ge(s_wlo, 2 * KC)
                    pe.wait_ge(s_mtlo, u + 1)
                    product(z_ps[c % 2], mt_hi[:, c % 2, :, :], mt_lo[:, c % 2, :, :], wg_hi, wg_lo, KC, False, True).then_inc(s_z, 1)
                if prev:
                    pe.wait_ge(s_hg, u)
                    transpose_rows(t13_ps, hid[:, :, :].rearrange("p x f -> p (x f)")).then_inc(s_ht, 1)
                    pe.wait_ge(s_rt, ROUTE_STEPS * u)
                    nc.tensor.transpose(r_ps[0:3 * X, 256:256 + P], gate_parts[:, :, :].rearrange("p a x -> p (a x)"),
                                        ident[:, :]).then_inc(s_gt, 1)
                if nx1:
                    if isinstance(k, int) and c == -1:
                        pe.wait_ge(s_wlo, KC)
                    pe.wait_ge(s_xtlo, u + 2)
                    at_least(pe, s_x1, u)
                    product(z_ps[(c + 1) % 2], xt_hi, xt_lo, wg_hi, wg_lo, 0, True, False).then_inc(s_zx, 1)
                if prev:
                    if isinstance(k, int) and c == 1:
                        pe.wait_ge(s_wlo, 4 * KC)
                    pe.wait_ge(s_htlo, u)
                    at_least(pe, s_out, u - 1)
                    pe.wait_ge(s_gtc, u)
                    nc.tensor.matmul(y_ps[:, :], gt_rows[:, :], b2_rows[:, :], start=True, stop=False)
                    product(y_ps, ht_hi, ht_lo, w2_hi, w2_lo, 0, False, True).then_inc(s_y, 1)
                if cur:
                    pe.wait_ge(s_xn2, u + 1)
                    at_least(pe, s_x2lo, u)
                    transpose_rows(t2_ps, xn2[:, :]).then_inc(s_x2t, 1)
                if nx2:
                    pe.wait_ge(s_xn, v + 1)
                    at_least(pe, s_htlo, u)
                    at_least(pe, s_xtlo, v)
                    transpose_rows(t13_ps, xn[:, :]).then_inc(s_xt, 1)
                    at_least(pe, s_mtlo, v)
                    sum_item(items_to(pe, further, v), 0, True)
                    more_items(pe, v, items, c + 2, lambda n: sum_item(n, 1, False), further, None, two_items)
                if cur:
                    if isinstance(k, int) and c == 0:
                        pe.wait_ge(s_wlo, 3 * KC)
                        pe.wait_ge(s_pre, 35)
                    pe.wait_ge(s_x2lo, u + 1)
                    at_least(pe, s_gtc, u)
                    for part in (x2t_hi, x2t_lo):
                        for c_ in range(KC):
                            last = nc.tensor.matmul(r_ps[0:2 * X, 0:P], wr[:, c_, :], part[:, c_, :],
                                                    start=(part is x2t_hi and c_ == 0), stop=(part is x2t_lo and c_ == KC - 1))
                    last.then_inc(s_lgt, 1)
                    at_least(pe, s_hg, u)
                    nc.tensor.matmul(h_ps[:, :], ones2[:, :], b1_rows[:, :], start=True, stop=False)
                    for c_ in range(KC):
                        if c_ == KC - 1:
                            pe.wait_ge(s_lgc, u + 1)
                        nc.tensor.matmul(h_ps[:, :], x2t_hi[:, c_, :], w1_hi[:, c_, :], start=False, stop=False)
                    nc.tensor.transpose(r_ps[:, 128:128 + 2 * X], lgt[:, :], ident[0:2 * X, 0:2 * X]).then_inc(s_lg, 1)
                    for c_ in range(KC):
                        nc.tensor.matmul(h_ps[:, :], x2t_hi[:, c_, :], w1_lo[:, c_, :], start=False, stop=False)
                        last = nc.tensor.matmul(h_ps[:, :], x2t_lo[:, c_, :], w1_hi[:, c_, :], start=False, stop=(c_ == KC - 1))
                    last.then_inc(s_h, 1)

            pe.wait_ge(s_pre, 24)
            periods(pe, period)

        @block.vector
        def _(dve):
            def upto(n):
                dve.wait_ge(s_pre, n)

            dve.wait_ge(s_const, 17)
            dve.wait_ge(s_dst, 32)
            dve.tensor_scalar(hi_i[:, :], dst_all[:, :], 7, None, op0=ALU.arith_shift_right).then_inc(s_pre, 1)
            dve.tensor_scalar(lo_i[:, :], dst_all[:, :], P - 1, None, op0=ALU.bitwise_and).then_inc(s_pre, 1)
            dve.tensor_copy(iota16[:, :], iota_i[:, :]).then_inc(s_pre, 1)
            upto(1)
            dve.tensor_copy(dst_tile[:, :], hi_i[:, :]).then_inc(s_pre, 1)
            upto(2)
            dve.tensor_copy(dst_node[:, :], lo_i[:, :]).then_inc(s_pre, 1)
            upto(5)
            dve.tensor_tensor(in_tile[:, :, :], dst_tile[:, :].unsqueeze(2).broadcast_to((P, EC, TILES)),
                              iota16[:, 0:TILES].unsqueeze(1).broadcast_to((P, EC, TILES)), op=ALU.is_equal).then_inc(s_pre, 1)
            dve.tensor_tensor(in_node[:, :, :], dst_node[:, :].unsqueeze(2).broadcast_to((P, EC, P)),
                              iota16[:, :].unsqueeze(1).broadcast_to((P, EC, P)), op=ALU.is_equal).then_inc(s_pre, 1)
            dve.tensor_copy(iota[:, :], iota_i[:, :]).then_inc(s_pre, 1)
            dve.tensor_copy(deg_tab[:, P:P + 1], base_i[:, :]).then_inc(s_pre, 1)
            dve.wait_ge(s_pairs, 32)
            dve.tensor_tensor(falls[:, :], dst_a[:, :], dst_b[:, :], op=ALU.is_gt).then_inc(s_pre, 1)
            upto(10)
            dve.tensor_reduce(fall[:, :], falls[:, :], axis=AX.X, op=ALU.add).then_inc(s_pre, 1)
            dve.wait_ge(s_hist, 1)
            dve.tensor_reduce(count[:, :], r_ps[0:TILES, 0:P], axis=AX.X, op=ALU.add).then_inc(s_pre, 1)
            dve.tensor_scalar(degree[:, :], r_ps[0:TILES, 0:P], 1.0, None, op0=ALU.max).then_inc(s_pre, 1)
            upto(13)
            dve.reciprocal(deg_tab[:, 0:P], degree[:, :]).then_inc(s_pre, 1)
            dve.wait_ge(s_span, 2)
            dve.tensor_copy(span[:, :, :], m_ps[0:1, 0:2 * TILES].rearrange("p (a t) -> p a t", a=2)).then_inc(s_pre, 1)
            dve.tensor_scalar(unsorted[:, :], m_ps[0:1, 256:257], 1.0, None, op0=ALU.min).then_inc(s_pre, 1)
            upto(16)
            dve.tensor_scalar(is_sorted[:, :], unsorted[:, :], -1.0, 1.0, op0=ALU.mult, op1=ALU.add).then_inc(s_pre, 1)
            dve.tensor_scalar(items_i[:, :], span[:, 1, :], float(P - 1), None, op0=ALU.add).then_inc(s_pre, 1)
            upto(18)
            dve.tensor_scalar(items_s[:, :], items_i[:, :], 7, None, op0=ALU.arith_shift_right).then_inc(s_pre, 1)
            upto(19)
            dve.tensor_scalar(items_f[:, :], items_s[:, :], 1.0, None, op0=ALU.max).then_inc(s_pre, 1)
            upto(20)
            dve.tensor_scalar(more[:, :], items_f[:, :], -1.0, float(ALL_ITEMS), op0=ALU.mult, op1=ALU.add).then_inc(s_pre, 1)
            upto(21)
            dve.scalar_tensor_tensor(more[:, :], more[:, :], unsorted[:, 0:1], items_f[:, :],
                                     op0=ALU.mult, op1=ALU.add).then_inc(s_pre, 1)
            dve.tensor_scalar(plan[:, 0, :], span[:, 0, :], is_sorted[:, 0:1], None, op0=ALU.mult).then_inc(s_pre, 1)
            upto(22)
            dve.tensor_copy(plan[:, 1, :], more[:, :]).then_inc(s_pre, 1)
            dve.wait_ge(s_small, 16 * 7)
            dve.tensor_copy(b2_hi[:, :].bitcast(F32R), b2_stage[:, :]).then_inc(s_pre, 1)
            dve.tensor_copy(b1_hi[:, :].bitcast(F32R), b1_stage[:, :]).then_inc(s_pre, 1)
            dve.tensor_copy(wr[:, :, 0:X], wr_stage[:, :, :]).then_inc(s_pre, 1)
            upto(27)
            dve.tensor_tensor(b2_lo[:, :], b2_stage[:, :], b2_hi[:, :], op=ALU.subtract).then_inc(s_pre, 1)
            dve.tensor_tensor(b1_lo[:, :], b1_stage[:, :], b1_hi[:, :], op=ALU.subtract).then_inc(s_pre, 1)
            dve.tensor_tensor(wr[:, :, X:2 * X], wr_stage[:, :, :], f32(wr[:, :, 0:X]), op=ALU.subtract).then_inc(s_pre, 1)
            dve.tensor_scalar(b2_hi[:, :], b2_hi[:, :], is_hi[:, 0:1], None, op0=ALU.mult).then_inc(s_pre, 1)
            dve.tensor_scalar(b1_hi[:, :], b1_hi[:, :], is_hi[0:2, 1:2], None, op0=ALU.mult).then_inc(s_pre, 1)
            upto(32)
            dve.scalar_tensor_tensor(b2_rows[:, :], b2_lo[:, :], is_lo[:, 0:1], b2_hi[:, :], op0=ALU.mult, op1=ALU.add).then_inc(s_pre, 1)
            dve.scalar_tensor_tensor(b1_rows[:, :], b1_lo[:, :], is_lo[0:2, 1:2], b1_hi[:, :], op0=ALU.mult, op1=ALU.add).then_inc(s_pre, 1)
            dve.tensor_copy(ones2[:, :], ones[0:2, :]).then_inc(s_pre, 1)
            dve.memset(weight[:, 0:1], 1.0 / MSG_SCALE).then_inc(s_pre, 1)
            upto(36)

            further = dve.alloc_register("dve_further")
            pairs = dve.alloc_register("dve_pairs")
            dve.reg_mov(further, 0)
            dve.reg_mov(pairs, 0)

            def edge_part(n, slot, rd, a, loads, first, lanes, between):
                base = n * EDGE_STEPS

                def step(i):
                    dve.wait_ge(s_es, base + i)

                dve.wait_ge(s_edge[slot], loads)
                dve.tensor_scalar(rel[:, :], edge[:, slot, a, 1:2], rdeg[:, rd, P:P + 1], None,
                                  op0=ALU.subtract).then_inc(s_es, 1)
                dve.wait_ge(s_raw[slot][a], loads)
                dve.bn_stats(stat_e[:, :], raw[:, slot, a, :]).then_inc(s_es, 1)
                step(1)
                at_least(dve, s_sum, buffer_free(n, a, first))
                dve.tensor_scalar(onehot[:, a, :], iota[:, :], rel[:, 0:1], None, op0=ALU.is_equal).then_inc(s_es, 1)
                between(0)
                step(3)
                dve.scalar_tensor_tensor(weighted[:, :], onehot[:, a, :], 1.0, rdeg[:, rd, 0:P], op0=ALU.mult,
                                         op1=ALU.mult, accum_out=weight[:, 1:2]).then_inc(s_es, 1)
                between(1)
                wait_apart(dve, (s_es, base + 2))
                dve.bn_aggr(mv[:, 1, :], stat_e[:, :]).then_inc(s_es, 1)
                between(2)
                dve.wait_ge(s_guess, n + 1)
                dve.scalar_tensor_tensor(newton[:, lanes], guess[:, lanes], -0.5, guess[:, lanes],
                                         op0=ALU.mult, op1=ALU.mult).then_inc(s_es, 1)
                between(3)
                step(6)
                dve.scalar_tensor_tensor(newton[:, lanes], mv[:, lanes, 1], EPS, newton[:, lanes],
                                         op0=ALU.add, op1=ALU.mult).then_inc(s_es, 1)
                between(4)
                step(7)
                dve.scalar_tensor_tensor(rstd[:, lanes], newton[:, lanes], 1.5, guess[:, lanes],
                                         op0=ALU.add, op1=ALU.mult).then_inc(s_es, 1)
                between(5)
                step(8)
                at_least(dve, s_mhi, n)
                dve.scalar_tensor_tensor(scale[:, lanes], rstd[:, lanes], MSG_SCALE, weight[:, lanes],
                                         op0=ALU.mult, op1=ALU.mult).then_inc(s_es, 1)
                between(6)
                step(9)
                dve.scalar_tensor_tensor(shift[:, lanes], mv[:, lanes, 0], -1.0, scale[:, lanes],
                                         op0=ALU.mult, op1=ALU.mult).then_inc(s_es, 1)
                between(7)

            def period(k, c):
                prev, cur, nx1, nx2, nx3 = known(k, c)
                u = tile_of(k, c)
                v = u + 2

                def norm2(n):
                    if not cur:
                        return
                    base = NORM2_STEPS * u
                    if n == 0:
                        dve.wait_ge(s_z, u + 1)
                        dve.scalar_tensor_tensor(x1[:, c % 2, :], z_ps[c % 2][:, :], 0.0, x_in[:, c % 4, :],
                                                 op0=ALU.max, op1=ALU.add).then_inc(s_x1, 1)
                    elif n == 1:
                        dve.wait_ge(s_x1, u + 1)
                        dve.bn_stats(stat2[:, :], x1[:, c % 2, :]).then_inc(s_n2, 1)
                    elif n == 2:
                        wait_apart(dve, (s_n2, base + 1))
                        dve.bn_aggr(mv2[:, :], stat2[:, :]).then_inc(s_n2, 1)
                    elif n == 3:
                        dve.wait_ge(s_n2, base + 2)
                        dve.wait_ge(s_guess2, u + 1)
                        dve.scalar_tensor_tensor(newton2[:, :], guess2[:, :], -0.5, guess2[:, :],
                                                 op0=ALU.mult, op1=ALU.mult).then_inc(s_n2, 1)
                    elif n == 4:
                        dve.wait_ge(s_n2, base + 3)
                        dve.scalar_tensor_tensor(newton2[:, :], mv2[:, 1:2], EPS, newton2[:, :],
                                                 op0=ALU.add, op1=ALU.mult).then_inc(s_n2, 1)
                    elif n == 5:
                        dve.wait_ge(s_n2, base + 4)
                        at_least(dve, s_xn2, u)
                        dve.scalar_tensor_tensor(rstd2[:, :], newton2[:, :], 1.5, guess2[:, :],
                                                 op0=ALU.add, op1=ALU.mult).then_inc(s_n2, 1)
                    elif n == 6:
                        dve.wait_ge(s_n2, base + 5)
                        dve.scalar_tensor_tensor(shift2[:, :], mv2[:, 0:1], -1.0, rstd2[:, :],
                                                 op0=ALU.mult, op1=ALU.mult).then_inc(s_n2, 1)

                def hidden_lo():
                    if prev:
                        dve.wait_ge(s_hthi, u)
                        at_least(dve, s_y, u - 1)
                        dve.tensor_tensor(ht_lo[:, :, :], t13_ps[:, :].rearrange("p (c n) -> p c n", c=KC),
                                          f32(ht_hi[:, :, :]), op=ALU.subtract).then_inc(s_htlo, 1)

                if prev:
                    dve.wait_ge(s_h, u)
                    at_least(dve, s_ht, u - 1)
                    dve.scalar_tensor_tensor(hid[:, :, :], h_ps[:, :].rearrange("p (x f) -> p x f", x=X), 0.0,
                                             gate[:, :].unsqueeze(2).broadcast_to((P, X, F)),
                                             op0=ALU.max, op1=ALU.mult).then_inc(s_hg, 1)
                if nx2:
                    items = dve.value_load(plan[0:1, 1, bass.ds(v, 1)], min_val=1, max_val=ALL_ITEMS)
                    n = items_to(dve, further, v)
                    dve.wait_ge(s_x[(c + 2) % 4], 16 * (uses(k, c + 2, 4) + 1))
                    dve.bn_stats(stat[:, :], x_in[:, (c + 2) % 4, :]).then_inc(s_norm, 1)
                    dve.wait_ge(s_rdeg[c % 2], 16 * (uses(k, c + 2, 2) + 1))

                    def between(i):
                        if i == 0:
                            norm2(0)
                        elif i == 1:
                            wait_apart(dve, (s_norm, NORM_STEPS * v + 1))
                            dve.bn_aggr(mv[:, 0, :], stat[:, :]).then_inc(s_norm, 1)
                        elif i == 2:
                            norm2(1)
                            norm2(2)
                            dve.wait_ge(s_norm, NORM_STEPS * v + 2)
                        elif i == 3:
                            hidden_lo()
                        elif i < 8:
                            norm2(i - 1)

                    edge_part(n, c % 2, c % 2, 0, 16 * (uses(k, c + 2, 2) + 1), True,
                              slice(0, 2), between)

                    def item(n, slot, a, loads):
                        edge_part(n, slot, c % 2, a, loads, False, slice(1, 2), lambda i: None)

                    def two_items(j, n, turns):
                        for a in range(ITEMS):
                            item(n + a, 2, a, (turns + 1) * 16)

                    more_items(dve, v, items, c + 2, lambda n: item(n, c % 2, 1, 16 * (uses(k, c + 2, 2) + 1)),
                               further, pairs, two_items)
                else:
                    hidden_lo()
                    for i in range(7):
                        norm2(i)
                if prev:
                    dve.wait_ge(s_y, u)
                    at_least(dve, s_st[(c - 1) % 2], 16 * uses(k, c - 1, 2))
                    dve.tensor_tensor(o_sb[:, (c - 1) % 2, :], y_ps[:, :], x1[:, (c - 1) % 2, :],
                                      op=ALU.add).then_inc(s_out, 1)
                if cur:
                    dve.wait_ge(s_x2hi, u + 1)
                    at_least(dve, s_h, u)
                    dve.tensor_tensor(x2t_lo[:, :, :], t2_ps[:, :].rearrange("p (c n) -> p c n", c=KC),
                                      f32(x2t_hi[:, :, :]), op=ALU.subtract).then_inc(s_x2lo, 1)
                if nx2:
                    dve.wait_ge(s_xthi, v + 1)
                    dve.tensor_tensor(xt_lo[:, :, :], t13_ps[:, :].rearrange("p (c n) -> p c n", c=KC),
                                      f32(xt_hi[:, :, :]), op=ALU.subtract).then_inc(s_xtlo, 1)
                if cur:
                    def routed(n):
                        dve.wait_ge(s_rt, ROUTE_STEPS * u + n)

                    dve.wait_ge(s_lg, u + 1)
                    at_least(dve, s_gt, u)
                    dve.tensor_reduce(lg[:, :], r_ps[:, 128:128 + 2 * X].rearrange("p (a x) -> p x a", a=2),
                                      axis=AX.X, op=ALU.add).then_inc(s_rt, 1)
                    routed(1)
                    dve.tensor_reduce(neg_max[:, :], lg[:, :], axis=AX.X, op=ALU.max, negate=True).then_inc(s_rt, 1)
                    dve.tensor_tensor(lg_diff[:, :, :], lg[:, :].unsqueeze(1).broadcast_to((P, X, X)),
                                      lg[:, :].unsqueeze(2).broadcast_to((P, X, X)), op=ALU.subtract).then_inc(s_rt, 1)
                    routed(3)
                    dve.tensor_tensor(beats[:, :, :], lg_diff[:, :, :], tie_bar[:, :, :], op=ALU.is_ge).then_inc(s_rt, 1)
                    routed(4)
                    dve.tensor_reduce(rank[:, :], beats[:, :, :], axis=AX.X, op=ALU.add).then_inc(s_rt, 1)
                if nx2:
                    dve.wait_ge(s_mthi, v + 1)
                    at_least(dve, s_z, u + 1)
                    dve.scalar_tensor_tensor(mt_lo[:, c % 2, :, :], m_ps[:, :].rearrange("p (c n) -> p c n", c=KC),
                                             1.0 / MSG_SCALE, f32(mt_hi[:, c % 2, :, :]), op0=ALU.mult,
                                             op1=ALU.subtract).then_inc(s_mtlo, 1)
                if cur:
                    dve.wait_ge(s_exp, u + 1)
                    dve.reciprocal(r_sum[:, :], ex_sum[:, :]).then_inc(s_rt, 1)
                    routed(5)
                    dve.scalar_tensor_tensor(ex_top[:, :], rank[:, :], 1.5, ex[:, :], op0=ALU.is_lt, op1=ALU.mult).then_inc(s_rt, 1)
                    routed(7)
                    dve.tensor_scalar(gate[:, :], ex_top[:, :], r_sum[:, 0:1], None, op0=ALU.mult).then_inc(s_rt, 1)
                    dve.tensor_scalar(gate_parts[:, 0:2, :].bitcast(F32R), ex_top[:, :].unsqueeze(1).broadcast_to((P, 2, X)),
                                      r_sum[:, 0:1], None, op0=ALU.mult).then_inc(s_rt, 1)
                    routed(9)
                    dve.tensor_tensor(gate_parts[:, 2, :], gate[:, :], gate_parts[:, 0, :], op=ALU.subtract).then_inc(s_rt, 1)

            periods(dve, period)

    return nc


_OUT = ((10000, 512), "float32")


def kernel(x, src, dst, L0_gnn_w, L0_ffn_Wr, L0_ffn_br, L0_ffn_W1, L0_ffn_b1, L0_ffn_W2, L0_ffn_b2):
    import numpy as np
    import concourse.bacc as bacc
    from concourse.bass_utils import run_bass_kernel_spmd

    w1 = np.asarray(L0_ffn_W1)
    w2 = np.asarray(L0_ffn_W2)
    X, D, F = w1.shape
    arrays = {
        "x": np.asarray(x),
        "edges": np.stack([np.asarray(src), np.asarray(dst)], axis=1),
        "dst": np.asarray(dst),
        "w_gnn": np.asarray(L0_gnn_w).T,
        "w_router": np.asarray(L0_ffn_Wr),
        "b_router": np.asarray(L0_ffn_br),
        "w1": w1.transpose(1, 0, 2).reshape(D, X * F),
        "b1": np.asarray(L0_ffn_b1).reshape(X * F),
        "w2": w2.reshape(X * F, D),
        "b2": np.asarray(L0_ffn_b2),
    }
    nc = bacc.Bacc("TRN2", target_bir_lowering=False, num_devices=1)
    feed, args = {}, []
    for name, a in arrays.items():
        a = np.ascontiguousarray(a)
        feed[f"in_{name}"] = a
        args.append(nc.dram_tensor(f"in_{name}", a.shape, mybir.dt.from_np(a.dtype), kind="ExternalInput").ap())
    shape, dtype = _OUT
    args.append(nc.dram_tensor("out_0", shape, mybir.dt.from_np(np.dtype(dtype)), kind="ExternalOutput").ap())
    moe_gnn_kernel(nc, *args)
    r = run_bass_kernel_spmd(nc, [feed], core_ids=[0])
    return r.results[0]["out_0"]
```

```python
from contextlib import ExitStack

import concourse.bass as bass
from concourse import mybir
from concourse.bass import OrderedEngineSet

F32 = mybir.dt.float32
F32R = mybir.dt.float32r
F16 = mybir.dt.float16
I32 = mybir.dt.int32
ALU = mybir.AluOpType
ACT = mybir.ActivationFunctionType
AX = mybir.AxisListType

P = 128
ITEMS = 2
TRIP = ITEMS * P
UNROLL = 4
EPS = 1e-5
MSG_SCALE = 2048.0
TIE = 1.2e-38
LANES = 1 + ITEMS
NORM_STEPS = 2
EDGE_STEPS = 14
NORM2_STEPS = 6
ROUTE_STEPS = 10


def tile_of(k, c):
    return UNROLL * k + c


def uses(k, c, slots):
    return UNROLL // slots * k + c // slots


def moe_gnn_kernel(nc, x, edges, dst, w_gnn, w_router, b_router, w1, b1, w2, b2, out):
    N, D = x.shape
    E = dst.shape[0]
    KC = D // P
    X = b_router.shape[0]
    F = w1.shape[1] // X
    H = X * F
    TILES = -(-N // P)
    TAIL = N - (TILES - 1) * P
    EC = -(-E // P)
    EP = E // EC
    ER = E - EP * EC
    ALL_ITEMS = -(-E // P)
    E_PAD = E + TRIP
    SP_ = 99
    SC = (E - 1) // SP_
    assert SP_ * SC == E - 1 and D == 4 * P and H == D and X == 8
    assert P == 1 << 7

    edge_list = nc.dram_tensor("edge_list", (E_PAD, 2), I32, kind="Internal").ap()
    deg_rows = nc.dram_tensor("deg_rows", (TILES, P + 1), F32, kind="Internal").ap()

    ctx = ExitStack()
    with ctx:
        def sb(name, shape, dt=F32):
            return ctx.enter_context(nc.sbuf_tensor(name, shape, dt))

        def pb(name, dt=F32):
            return ctx.enter_context(nc.psum_tensor(name, [P, 512], dt))

        def sem(name):
            return ctx.enter_context(nc.semaphore(name))

        w_stage = sb("w_stage", [P, 2 * KC, D])
        wr_stage = sb("wr_stage", [P, KC, X])
        wg_hi = sb("wg_hi", [P, 2 * KC, D], F32R)
        wg_lo = sb("wg_lo", [P, 2 * KC, D], F32R)
        w1_hi = sb("w1_hi", [P, KC, H], F32R)
        w1_lo = sb("w1_lo", [P, KC, H], F32R)
        w2_hi = sb("w2_hi", [P, KC, D], F32R)
        w2_lo = sb("w2_lo", [P, KC, D], F32R)
        wr = sb("wr", [P, KC, 2 * X], F32R)
        br16 = sb("br16", [2 * X, 1])
        b2_stage = sb("b2_stage", [3 * X, D])
        b2_hi = sb("b2_hi", [3 * X, D])
        b2_lo = sb("b2_lo", [3 * X, D])
        b2_rows = sb("b2_rows", [3 * X, D], F32R)
        b1_stage = sb("b1_stage", [2, H])
        b1_hi = sb("b1_hi", [2, H])
        b1_lo = sb("b1_lo", [2, H])
        b1_rows = sb("b1_rows", [2, H], F32R)
        ones2 = sb("ones2", [2, P], F32R)
        is_lo = sb("is_lo", [3 * X, 2])
        is_hi = sb("is_hi", [3 * X, 2])
        ones = sb("ones", [P, P])
        ident = sb("ident", [P, P])
        iota_i = sb("iota_i", [P, P], I32)
        iota = sb("iota", [P, P])
        iota16 = sb("iota16", [P, P], F16)
        eps_col = sb("eps_col", [P, 1])
        tie_bar = sb("tie_bar", [P, X, X])
        dst_all = sb("dst_all", [P, EC], I32)
        hi_i = sb("hi_i", [P, EC], I32)
        lo_i = sb("lo_i", [P, EC], I32)
        dst_tile = sb("dst_tile", [P, EC], F16)
        dst_node = sb("dst_node", [P, EC], F16)
        in_tile = sb("in_tile", [P, EC, TILES], F16)
        in_node = sb("in_node", [P, EC, P], F16)
        pad_rows = sb("pad_rows", [P, (E_PAD - E) // P, 2], I32)
        deg_tab = sb("deg_tab", [TILES, P + 1])
        degree = sb("degree", [TILES, P])
        count = sb("count", [TILES, 1])
        base_i = sb("base_i", [TILES, 1], I32)
        before = sb("before", [TILES, 2 * TILES])
        dst_a = sb("dst_a", [SP_, SC], I32)
        dst_b = sb("dst_b", [SP_, SC], I32)
        falls = sb("falls", [SP_, SC])
        fall = sb("fall", [SP_, 1])
        unsorted = sb("unsorted", [1, 1])
        is_sorted = sb("is_sorted", [1, 1])
        span = sb("span", [1, 2, TILES])
        items_i = sb("items_i", [1, TILES], I32)
        items_s = sb("items_s", [1, TILES], I32)
        items_f = sb("items_f", [1, TILES])
        more = sb("more", [1, TILES])
        plan = sb("plan", [1, 2, TILES], I32)
        x_in = sb("x_in", [P, 4, D])
        rdeg = sb("rdeg", [P, 4, P + 1])
        stat = sb("stat", [P, 6])
        mv = sb("mv", [P, LANES, 2])
        ln_v = sb("ln_v", [P, LANES])
        guess = sb("guess", [P, LANES])
        newton = sb("newton", [P, LANES])
        rstd = sb("rstd", [P, LANES])
        weight = sb("weight", [P, LANES])
        scale = sb("scale", [P, LANES])
        shift = sb("shift", [P, LANES])
        xn = sb("xn", [P, D])
        xt_hi = sb("xt_hi", [P, KC, P], F32R)
        xt_lo = sb("xt_lo", [P, KC, P], F32R)
        mt_hi = sb("mt_hi", [P, 2, KC, P], F32R)
        mt_lo = sb("mt_lo", [P, 2, KC, P], F32R)
        x1 = sb("x1", [P, 2, D])
        stat2 = sb("stat2", [P, 6])
        mv2 = sb("mv2", [P, 2])
        ln_v2 = sb("ln_v2", [P, 1])
        guess2 = sb("guess2", [P, 1])
        newton2 = sb("newton2", [P, 1])
        rstd2 = sb("rstd2", [P, 1])
        shift2 = sb("shift2", [P, 1])
        xn2 = sb("xn2", [P, D])
        x2t_hi = sb("x2t_hi", [P, KC, P], F32R)
        x2t_lo = sb("x2t_lo", [P, KC, P], F32R)
        lgt = sb("lgt", [2 * X, P])
        lg = sb("lg", [P, X])
        neg_max = sb("neg_max", [P, 1])
        lg_diff = sb("lg_diff", [P, X, X])
        beats = sb("beats", [P, X, X])
        rank = sb("rank", [P, X])
        ex = sb("ex", [P, X])
        ex_sum = sb("ex_sum", [P, 1])
        r_sum = sb("r_sum", [P, 1])
        ex_top = sb("ex_top", [P, X])
        gate = sb("gate", [P, X])
        gate_parts = sb("gate_parts", [P, 3, X])
        gt_rows = sb("gt_rows", [3 * X, P], F32R)
        hid = sb("hid", [P, X, F])
        ht_hi = sb("ht_hi", [P, KC, P], F32R)
        ht_lo = sb("ht_lo", [P, KC, P], F32R)
        o_sb = sb("o_sb", [P, 2, D])
        edge = sb("edge", [P, 4, ITEMS, 2], I32)
        edge_further = sb("edge_further", [P, 2, ITEMS, 2], I32)
        raw = in_node[:, :, :].rearrange("p c n -> p (c n)").bitcast(F32)[:, 0:4 * ITEMS * D].rearrange(
            "p (s a d) -> p s a d", s=4, a=ITEMS)
        rel = sb("rel", [P, ITEMS])
        onehot = sb("onehot", [P, 2 * ITEMS, P], F16)
        weighted = sb("weighted", [P, ITEMS, P])
        stat_e = sb("stat_e", [P, ITEMS, 6])
        msg = sb("msg", [P, ITEMS, D])
        msg_hi = sb("msg_hi", [P, ITEMS, D], F16)
        msg_lo = sb("msg_lo", [P, ITEMS, D], F16)

        z_ps = [pb("z0_ps"), pb("z1_ps")]
        h_ps = pb("h_ps")
        y_ps = pb("y_ps")
        t2_ps = pb("t2_ps")
        t13_ps = pb("t13_ps")
        m_ps = pb("m_ps")
        r_ps = pb("r_ps")

        s_dst = sem("dst_loaded")
        s_pairs = sem("sort_pairs_loaded")
        s_wg = [sem(f"wg_loaded{p}") for p in range(2)]
        s_w1 = sem("w1_loaded")
        s_w2 = sem("w2_loaded")
        s_small = sem("small_loaded")
        s_const = sem("pool_consts")
        s_pre = sem("vector_setup")
        s_block = sem("one_hot_blocks")
        s_hist = sem("histogram_done")
        s_span = sem("span_summed")
        s_deg = sem("deg_rows_stored")
        s_list = sem("edge_list_stored")
        s_apart = sem("waits_apart")
        s_whi = sem("weights_hi")
        s_wlo = sem("weights_lo")
        s_x = [sem(f"x_loaded{p}") for p in range(4)]
        s_rdeg = [sem(f"rdeg_loaded{p}") for p in range(4)]
        s_edge = [sem(f"edges_loaded{p}") for p in range(4)]
        s_further = [sem("second_edges_loaded"), sem("later_edges_loaded")]
        s_raw = [[sem(f"rows_gathered{p}{a}") for a in range(ITEMS)] for p in range(4)]
        s_norm = sem("norm_steps")
        s_xn = sem("xn_ready")
        s_xn2 = sem("xn2_ready")
        s_xt = sem("x_transposed")
        s_xthi = sem("xt_hi_ready")
        s_xtlo = sem("xt_lo_ready")
        s_es = sem("edge_steps")
        s_ln = sem("variance_logs")
        s_guess = sem("rstd_guessed")
        s_msg = sem("messages_normed")
        s_mhi = sem("messages_hi")
        s_mlo = sem("messages_lo")
        s_sum = sem("items_summed")
        s_mthi = sem("mean_hi_ready")
        s_mtlo = sem("mean_lo_ready")
        s_z = sem("gnn_done")
        s_x1 = sem("x1_ready")
        s_n2 = sem("norm2_steps")
        s_ln2 = sem("variance2_logs")
        s_guess2 = sem("rstd2_guessed")
        s_x2t = sem("x2_transposed")
        s_x2hi = sem("x2t_hi_ready")
        s_x2lo = sem("x2t_lo_ready")
        s_lgt = sem("logits_done")
        s_lgc = sem("logits_copied")
        s_lg = sem("logits_transposed")
        s_rt = sem("route_steps")
        s_exp = sem("exp_ready")
        s_gt = sem("gate_transposed")
        s_gtc = sem("gate_rows_ready")
        s_h = sem("hidden_done")
        s_hg = sem("hidden_gated")
        s_ht = sem("hidden_transposed")
        s_hthi = sem("ht_hi_ready")
        s_htlo = sem("ht_lo_ready")
        s_y = sem("ffn_done")
        s_out = sem("out_ready")
        s_st = [sem(f"out_stored{p}") for p in range(2)]

        block = ctx.enter_context(nc.Block())

        def f32(ap):
            return ap.bitcast(F32)

        blocks = [(EC * b // 4, EC * (b + 1) // 4) for b in range(4)]

        def at_least(eng, s, value):
            if not isinstance(value, int) or value > 0:
                eng.wait_ge(s, value)

        def wait_apart(eng, *waits):
            for s, n in waits:
                at_least(eng, s, n)
            eng.sem_inc(s_apart, 1)

        def periods(eng, period):
            first = 3
            last = first + (TILES - 5 - first) // UNROLL * UNROLL
            for u in range(-4, first):
                period(0, u)
            with nc.Fori(0, (last - first) // UNROLL, engines=OrderedEngineSet([eng.engine]), hint_back_edge=True) as k:
                for i in range(UNROLL):
                    period(k, first + i)
            for u in range(last, TILES + 1):
                period(0, u)

        def known(k, c):
            looped = not isinstance(k, int)
            return [looped or 0 <= c + i < TILES for i in (-1, 0, 1, 2, 3, 4)]

        def items_to(eng, further, v):
            return 0 if isinstance(v, int) and v == 0 else eng.snap(further) + v

        def buffer_free(n, first):
            return n if first else n - 1

        def second_item(eng, v, count, further, item):
            if item is not None:
                item(v + 1 if count == 0 else eng.snap(further) + (v + 1))
            eng.reg_add(further, further, 1)

        def more_trips(eng, v, items, further, in_second, in_later, second_trip, later_trip):
            with eng.If(items > ITEMS):
                second_trip(eng.snap(further) + (v + 1))
                eng.reg_add(further, further, ITEMS)
                for register in in_second:
                    eng.reg_add(register, register, 1)
                with eng.If(items > 2 * ITEMS):
                    with eng.Fori(2 * ITEMS, items, ITEMS) as j:
                        later_trip(j, eng.snap(further) + (v + 1))
                        eng.reg_add(further, further, ITEMS)
                        for register in in_later:
                            eng.reg_add(register, register, 1)

        def more_items(eng, v, items, count, further, in_second, in_later, item, second_trip, later_trip):
            with eng.If(items > 1):
                second_item(eng, v, count, further, item)
                more_trips(eng, v, items, further, in_second, in_later, second_trip, later_trip)

        def rows_of(k, c):
            return P if not isinstance(k, int) or c < TILES - 1 else TAIL

        @block.sync
        def _(sync):
            sync.wait_ge(s_const, 1)
            sync.dma_start(dst_all[0:EP, :], dst[0:EP * EC].rearrange("(p c) -> p c", c=EC)).then_inc(s_dst, 16)
            sync.dma_start(dst_a[:, :], dst[0:E - 1].rearrange("(p c) -> p c", c=SC)).then_inc(s_pairs, 16)
            sync.dma_start(dst_b[:, :], dst[1:E].rearrange("(p c) -> p c", c=SC)).then_inc(s_pairs, 16)
            sync.dma_start(edge_list[0:E, :].rearrange("(q r) c -> q (r c)", q=16),
                           edges.rearrange("(q r) c -> q (r c)", q=16)).then_inc(s_list, 16)
            sync.wait_ge(s_const, 3)
            sync.dma_start(edge_list[E:E_PAD, :].rearrange("(p r) c -> p r c", p=P),
                           pad_rows[:, :, :]).then_inc(s_list, 16)
            wg_v = w_gnn.rearrange("(c p) n -> p c n", p=P)
            sync.dma_start(w_stage[:, 0:KC, :], wg_v[:, 0:KC, :]).then_inc(s_wg[0], 16)

            def load_x(k, c):
                n = rows_of(k, c)
                sync.dma_start(x_in[0:n, c % 4, :], x[bass.ds(tile_of(k, c) * P, n), :]).then_inc(s_x[c % 4], 16)

            def load_edges(k, c):
                t = tile_of(k, c)
                start = sync.value_load(plan[0:1, 0, bass.ds(t, 1)], min_val=0, max_val=E)
                sync.dma_start(edge[:, c % 4, :, :],
                               edge_list[bass.ds(start, TRIP), :].rearrange("(a p) c -> p a c", a=ITEMS)
                               ).then_inc(s_edge[c % 4], 16)
                if isinstance(k, int) and c == 0:
                    sync.wait_ge(s_deg, 16)
                sync.dma_start(rdeg[:, c % 4, :], deg_rows[bass.ds(t, 1), :].broadcast_to((P, P + 1))
                               ).then_inc(s_rdeg[c % 4], 16)

            for t in range(4):
                load_x(0, t)
            sync.dma_start(w_stage[:, KC:2 * KC, :], wg_v[:, KC:2 * KC, :]).then_inc(s_wg[1], 16)
            sync.wait_ge(s_wlo, KC)
            sync.dma_start(w_stage[:, 0:KC, :], w1.rearrange("(c p) n -> p c n", p=P)).then_inc(s_w1, 16)
            sync.wait_ge(s_wlo, 2 * KC)
            sync.dma_start(w_stage[:, KC:2 * KC, :], w2.rearrange("(c p) n -> p c n", p=P)).then_inc(s_w2, 16)
            sync.wait_ge(s_pre, 22)
            sync.dma_start(deg_rows[:, :], deg_tab[:, :]).then_inc(s_deg, 16)
            sync.wait_ge(s_list, 32)

            def period(k, c):
                prev, cur, nx1, nx2, nx3, nx4 = known(k, c)
                u = tile_of(k, c)
                if nx4:
                    at_least(sync, s_mthi, u + 1)
                    load_edges(k, c + 4)
                    if cur:
                        sync.wait_ge(s_x1, u + 1)
                        load_x(k, c + 4)
                if prev:
                    n = rows_of(k, c - 1)
                    sync.wait_ge(s_out, u)
                    sync.dma_start(out[bass.ds((u - 1) * P, n), :], o_sb[0:n, (c - 1) % 2, :]).then_inc(s_st[(c - 1) % 2], 16)

            periods(sync, period)
            sync.wait_ge(s_st[0], 16 * ((TILES + 1) // 2))
            sync.wait_ge(s_st[1], 16 * (TILES // 2))

        @block.gpsimd
        def _(pool):
            pool.memset(dst_all[:, :], -1).then_inc(s_const, 1)
            pool.memset(pad_rows[:, :, 0:1], 0).then_inc(s_const, 1)
            pool.memset(pad_rows[:, :, 1:2], -1).then_inc(s_const, 1)
            pool.iota(iota_i[:, :], pattern=[[1, P]], base=0, channel_multiplier=0).then_inc(s_const, 1)
            pool.iota(base_i[:, :], pattern=[[0, 1]], base=0, channel_multiplier=P).then_inc(s_const, 1)
            pool.memset(ones[:, :], 1.0).then_inc(s_const, 1)
            pool.memset(br16[:, :], 0.0).then_inc(s_const, 1)
            pool.memset(eps_col[:, :], EPS).then_inc(s_const, 1)
            pool.wait_ge(s_const, 8)
            pool.affine_select(out=ident[:, :], in_=ones[:, :], compare_op=ALU.is_equal, fill=0.0,
                               base=0, pattern=[[-1, P]], channel_multiplier=1).then_inc(s_const, 1)
            pool.affine_select(out=before[:, 0:TILES], in_=ones[0:TILES, 0:TILES], compare_op=ALU.is_gt, fill=0.0,
                               base=0, pattern=[[1, TILES]], channel_multiplier=-1).then_inc(s_const, 1)
            pool.affine_select(out=before[:, TILES:2 * TILES], in_=ones[0:TILES, 0:TILES], compare_op=ALU.is_equal,
                               fill=0.0, base=0, pattern=[[1, TILES]], channel_multiplier=-1).then_inc(s_const, 1)
            pool.memset(tie_bar[:, :, :], TIE).then_inc(s_const, 1)
            pool.affine_select(out=is_lo[:, 0:1], in_=ones[0:3 * X, 0:1], compare_op=ALU.is_ge, fill=0.0,
                               base=-X, pattern=[[0, 1]], channel_multiplier=1).then_inc(s_const, 1)
            pool.affine_select(out=is_lo[:, 1:2], in_=ones[0:3 * X, 0:1], compare_op=ALU.is_ge, fill=0.0,
                               base=-1, pattern=[[0, 1]], channel_multiplier=1).then_inc(s_const, 1)
            pool.wait_ge(s_const, 14)
            pool.affine_select(out=tie_bar[:, :, :], in_=tie_bar[:, :, :], compare_op=ALU.is_ge, fill=0.0,
                               base=0, pattern=[[-1, X], [1, X]], channel_multiplier=0).then_inc(s_const, 1)
            pool.affine_select(out=is_lo[:, 0:1], in_=is_lo[:, 0:1], compare_op=ALU.is_ge, fill=0.0,
                               base=2 * X - 1, pattern=[[0, 1]], channel_multiplier=-1).then_inc(s_const, 1)
            pool.wait_ge(s_const, 16)
            pool.tensor_scalar(is_hi[:, :], is_lo[:, :], -1.0, 1.0, op0=ALU.mult, op1=ALU.add).then_inc(s_const, 1)

            chunks = [(wg_lo, wg_hi, c, c) for c in range(2 * KC)]
            chunks += [(w1_lo, w1_hi, c, c) for c in range(KC)] + [(w2_lo, w2_hi, c, KC + c) for c in range(KC)]
            for n, (lo, hi, c, at) in enumerate(chunks):
                pool.wait_ge(s_whi, n + 1)
                pool.tensor_tensor(lo[:, c, :], w_stage[:, at, :], f32(hi[:, c, :]), op=ALU.subtract).then_inc(s_wlo, 1)

            def gather(slot, edges, loaded, count):
                wait_apart(pool, (loaded, count))
                for a in range(ITEMS):
                    pool.indirect_dma_start(
                        out=raw[:, slot, a, :], out_offset=None, in_=x[:, :],
                        in_offset=bass.IndirectOffsetOnAxis(ap=edges[:, a, 0:1], axis=0),
                        bounds_check=N - 1, oob_is_err=False).then_inc(s_raw[slot][a], 16)

            further = pool.alloc_register("pool_further")
            fetched = [pool.alloc_register("pool_seconds"), pool.alloc_register("pool_laters")]
            pool.reg_mov(further, 0)
            for register in fetched:
                pool.reg_mov(register, 0)

            def load_further(v, which, place):
                start = pool.value_load(plan[0:1, 0, bass.ds(v, 1)], min_val=0, max_val=E)
                row = pool.snap(nc.s_assert_within(start + place * P, min_val=0, max_val=E,
                                                   skip_runtime_bounds_check_because="a trip starts before the last edge"))
                pool.dma_start(edge_further[:, which, :, :],
                               edge_list[bass.ds(row, TRIP), :].rearrange("(a p) c -> p a c", a=ITEMS)
                               ).then_inc(s_further[which], 16)

            def gather_further(which):
                gather(2 + which, edge_further[:, which, :, :], s_further[which], pool.snap(fetched[which]) * 16 + 16)
                pool.reg_add(fetched[which], fetched[which], 1)

            def message_lo(n, a, first):
                pool.wait_ge(s_msg, n + 1)
                pool.wait_ge(s_mhi, n + 1)
                at_least(pool, s_sum, buffer_free(n, first))
                pool.tensor_tensor(msg_lo[:, a, :], msg[:, a, :], msg_hi[:, a, :], op=ALU.subtract).then_inc(s_mlo, 1)

            pool.wait_ge(s_pre, 22)

            def period(k, c):
                prev, cur, nx1, nx2, nx3, nx4 = known(k, c)
                if nx2:
                    v = tile_of(k, c + 2)
                    items = pool.value_load(plan[0:1, 1, bass.ds(v, 1)], min_val=1, max_val=ALL_ITEMS)
                    message_lo(items_to(pool, further, v), 0, True)

                    def split(n):
                        for a in range(ITEMS):
                            message_lo(n + a, a, False)

                    def later_trip(j, n):
                        with pool.If(items - j > ITEMS):
                            trip = pool.snap(fetched[0]) + pool.snap(fetched[1]) + v
                            gathers = pool.snap(fetched[1]) * 16
                            wait_apart(pool, (s_es, trip * EDGE_STEPS + 1), *[(s_raw[3][a], gathers) for a in range(ITEMS)])
                            load_further(v, 1, j + ITEMS)
                            wait_apart(pool, (s_mhi, n + ITEMS))
                            gather_further(1)
                        split(n)

                    more_items(pool, v, items, c + 2, further, (), (),
                               lambda n: message_lo(n, 1, False), split, later_trip)
                if nx4:
                    gather(c % 2, edge[:, c % 4, :, :], s_edge[c % 4], 16 * (uses(k, c + 4, 4) + 1))
                if nx3:
                    w = tile_of(k, c + 3)
                    items = pool.value_load(plan[0:1, 1, bass.ds(w, 1)], min_val=1, max_val=ALL_ITEMS)
                    with pool.If(items > ITEMS):
                        load_further(w, 0, ITEMS)
                        gather_further(0)
                        with pool.If(items > 2 * ITEMS):
                            load_further(w, 1, 2 * ITEMS)
                            gather_further(1)

            periods(pool, period)

        @block.scalar
        def _(act):
            act.wait_ge(s_const, 1)
            act.dma_start(dst_all[EP:EP + 1, 0:ER], dst[EP * EC:E].rearrange("(p c) -> p c", p=1)).then_inc(s_dst, 16)
            act.dma_start(wr_stage[:, :, :], w_router.rearrange("(c p) n -> p c n", p=P)).then_inc(s_small, 16)
            act.wait_ge(s_const, 8)
            act.dma_start(br16[0:X, :], b_router.rearrange("(p c) -> p c", c=1)).then_inc(s_small, 16)
            for i in range(3):
                act.dma_start(b2_stage[i * X:(i + 1) * X, :], b2[:, :]).then_inc(s_small, 16)
            for i in range(2):
                act.dma_start(b1_stage[i:i + 1, :], b1.rearrange("(p c) -> p c", p=1)).then_inc(s_small, 16)
            chunks = [(wg_hi, c, c, s_wg[c // KC]) for c in range(2 * KC)]
            chunks += [(w1_hi, c, c, s_w1) for c in range(KC)] + [(w2_hi, c, KC + c, s_w2) for c in range(KC)]
            for hi, c, at, s in chunks:
                act.wait_ge(s, 16)
                act.activation(hi[:, c, :], w_stage[:, at, :], ACT.Copy).then_inc(s_whi, 1)

            further = act.alloc_register("act_further")
            act.reg_mov(further, 0)
            trips = act.alloc_register("act_trips")
            act.reg_mov(trips, 0)

            def guess_rstd(trip, lanes, tile=None):
                if tile is not None:
                    act.wait_ge(s_norm, NORM_STEPS * (tile + 1))
                act.wait_ge(s_es, trip * EDGE_STEPS + 7)
                act.activation(ln_v[:, lanes], mv[:, lanes, 1], ACT.Ln, bias=eps_col[:, 0:1]).then_inc(s_ln, 1)
                act.wait_ge(s_ln, trip + 1)
                act.activation(guess[:, lanes], ln_v[:, lanes], ACT.Exp, scale=-0.5).then_inc(s_guess, 1)

            def item_rows(n, slot, a, first):
                at_least(act, s_mlo, buffer_free(n, first))
                act.activation(msg[:, a, :], raw[:, slot, a, :], ACT.Identity, bias=shift[:, 1 + a:2 + a],
                               scale=scale[:, 1 + a:2 + a]).then_inc(s_msg, 1)

            def item_hi(n, slot, a, first):
                at_least(act, s_sum, buffer_free(n, first))
                act.activation(msg_hi[:, a, :], raw[:, slot, a, :], ACT.Identity, bias=shift[:, 1 + a:2 + a],
                               scale=scale[:, 1 + a:2 + a]).then_inc(s_mhi, 1)

            def second(n, slot):
                item_rows(n, slot, 1, False)
                item_hi(n, slot, 1, False)

            def trip(v, slot):
                def run(n):
                    t = act.snap(trips) + (v + 1)
                    guess_rstd(t, slice(1, LANES))
                    act.wait_ge(s_es, t * EDGE_STEPS + EDGE_STEPS)
                    for a in range(ITEMS):
                        item_rows(n + a, slot, a, False)
                        item_hi(n + a, slot, a, False)
                return run

            def period(k, c):
                prev, cur, nx1, nx2, nx3, nx4 = known(k, c)
                u = tile_of(k, c)
                v, w = u + 2, u + 3
                if nx2:
                    items = act.value_load(plan[0:1, 1, bass.ds(v, 1)], min_val=1, max_val=ALL_ITEMS)
                if prev:
                    act.wait_ge(s_ht, u)
                    at_least(act, s_y, u - 1)
                    act.activation(ht_hi[:, :, :], t13_ps[:, :].rearrange("p (c n) -> p c n", c=KC), ACT.Copy).then_inc(s_hthi, 1)
                    act.wait_ge(s_gt, u)
                    act.activation(gt_rows[:, :], r_ps[0:3 * X, 256:256 + P], ACT.Copy).then_inc(s_gtc, 1)
                if nx2:
                    with act.If(items > 1):
                        second_item(act, v, c + 2, further, lambda n: second(n, c % 2))
                if cur:
                    act.wait_ge(s_n2, NORM2_STEPS * u + 2)
                    act.activation(ln_v2[:, :], mv2[:, 1:2], ACT.Ln, bias=eps_col[:, 0:1]).then_inc(s_ln2, 1)
                    act.wait_ge(s_ln2, u + 1)
                    act.activation(guess2[:, :], ln_v2[:, :], ACT.Exp, scale=-0.5).then_inc(s_guess2, 1)
                    act.wait_ge(s_n2, NORM2_STEPS * u + 6)
                    at_least(act, s_x2t, u)
                    act.activation(xn2[:, :], x1[:, c % 2, :], ACT.Identity, bias=shift2[:, 0:1],
                                   scale=rstd2[:, 0:1]).then_inc(s_xn2, 1)
                if nx2:
                    more_trips(act, v, items, further, (trips,), (trips,), trip(v, 2), lambda j, n: trip(v, 3)(n))
                if cur:
                    act.wait_ge(s_x2t, u + 1)
                    at_least(act, s_h, u)
                    act.activation(x2t_hi[:, :, :], t2_ps[:, :].rearrange("p (c n) -> p c n", c=KC), ACT.Copy).then_inc(s_x2hi, 1)
                if nx2:
                    act.wait_ge(s_xt, v + 1)
                    act.activation(xt_hi[:, :, :], t13_ps[:, :].rearrange("p (c n) -> p c n", c=KC), ACT.Copy).then_inc(s_xthi, 1)
                if cur:
                    act.wait_ge(s_lgt, u + 1)
                    act.activation(lgt[:, :], r_ps[0:2 * X, 0:P], ACT.Identity, bias=br16[:, 0:1]).then_inc(s_lgc, 1)
                if nx3:
                    n = items_to(act, further, w)
                    t = items_to(act, trips, w)
                    guess_rstd(t, slice(0, LANES), w)
                if nx2:
                    act.wait_ge(s_sum, act.snap(further) + (v + 1))
                    at_least(act, s_z, u + 1)
                    act.activation(mt_hi[:, c % 2, :, :], m_ps[:, :].rearrange("p (c n) -> p c n", c=KC), ACT.Copy,
                                   scale=1.0 / MSG_SCALE).then_inc(s_mthi, 1)
                if cur:
                    act.wait_ge(s_rt, ROUTE_STEPS * u + 2)
                    act.activation(ex[:, :], lg[:, :], ACT.Exp, bias=neg_max[:, 0:1],
                                   accum_out=ex_sum[:, 0:1]).then_inc(s_exp, 1)
                if nx3:
                    act.wait_ge(s_es, t * EDGE_STEPS + EDGE_STEPS)
                    at_least(act, s_xt, w)
                    act.activation(xn[:, :], x_in[:, (c + 3) % 4, :], ACT.Identity, bias=shift[:, 0:1],
                                   scale=scale[:, 0:1]).then_inc(s_xn, 1)
                    item_rows(n, (c + 3) % 2, 0, True)
                    item_hi(n, (c + 3) % 2, 0, True)

            act.wait_ge(s_small, 16 * 7)
            act.preload_act_table_set("natural_log_exp_and_others")
            act.wait_ge(s_pre, 22)
            periods(act, period)

        @block.tensor
        def _(pe):
            for c in range(EC):
                for b, (c0, c1) in enumerate(blocks):
                    if c == c0:
                        pe.wait_ge(s_block, 2 * b + 2)
                last = nc.tensor.matmul(r_ps[0:TILES, 0:P], in_tile[:, c, :], in_node[:, c, :],
                                        start=(c == 0), stop=(c == EC - 1))
            last.then_inc(s_hist, 1)
            pe.wait_ge(s_const, 11)
            pe.wait_ge(s_pre, 10)
            nc.tensor.matmul(m_ps[0:1, 0:2 * TILES], count[:, :], before[:, :], start=True, stop=True).then_inc(s_span, 1)
            nc.tensor.matmul(m_ps[0:1, 256:257], fall[:, :], ones[0:SP_, 0:1], start=True, stop=True).then_inc(s_span, 1)

            further = pe.alloc_register("pe_further")
            pe.reg_mov(further, 0)

            def product(bank, hi, lo, w_hi, w_lo, w_from, start, stop):
                for c in range(KC):
                    nc.tensor.matmul(bank[:, :], hi[:, c, :], w_hi[:, w_from + c, :], start=start and c == 0, stop=False)
                    nc.tensor.matmul(bank[:, :], hi[:, c, :], w_lo[:, w_from + c, :], start=False, stop=False)
                    last = nc.tensor.matmul(bank[:, :], lo[:, c, :], w_hi[:, w_from + c, :], start=False,
                                            stop=stop and c == KC - 1)
                return last

            def sum_item(n, a, first, rows=0):
                pe.wait_ge(s_mlo, n + 1)
                for c in range(KC):
                    for part in (msg_hi, msg_lo):
                        last = nc.tensor.matmul(m_ps[:, c * P:(c + 1) * P], part[:, a, c * P:(c + 1) * P],
                                                onehot[:, rows + a, :], start=first and c == 0 and part is msg_hi,
                                                stop=False, skip_group_check=True)
                last.then_inc(s_sum, 1)

            def trip(n, rows):
                for a in range(ITEMS):
                    sum_item(n + a, a, False, rows)

            def transpose_rows(bank, rows):
                for c in range(KC):
                    last = nc.tensor.transpose(bank[:, c * P:(c + 1) * P], rows[:, c * P:(c + 1) * P], ident[:, :])
                return last

            def period(k, c):
                prev, cur, nx1, nx2, nx3, nx4 = known(k, c)
                u = tile_of(k, c)
                v = u + 2
                if nx2:
                    items = pe.value_load(plan[0:1, 1, bass.ds(v, 1)], min_val=1, max_val=ALL_ITEMS)
                if cur:
                    if isinstance(k, int) and c == 0:
                        pe.wait_ge(s_wlo, 2 * KC)
                    pe.wait_ge(s_mtlo, u + 1)
                    product(z_ps[c % 2], mt_hi[:, c % 2, :, :], mt_lo[:, c % 2, :, :], wg_hi, wg_lo, KC, False, True).then_inc(s_z, 1)
                if prev:
                    pe.wait_ge(s_hg, u)
                    transpose_rows(t13_ps, hid[:, :, :].rearrange("p x f -> p (x f)")).then_inc(s_ht, 1)
                    pe.wait_ge(s_rt, ROUTE_STEPS * u)
                    nc.tensor.transpose(r_ps[0:3 * X, 256:256 + P], gate_parts[:, :, :].rearrange("p a x -> p (a x)"),
                                        ident[:, :]).then_inc(s_gt, 1)
                if nx1:
                    if isinstance(k, int) and c == -1:
                        pe.wait_ge(s_wlo, KC)
                    pe.wait_ge(s_xtlo, u + 2)
                    at_least(pe, s_x1, u)
                    product(z_ps[(c + 1) % 2], xt_hi, xt_lo, wg_hi, wg_lo, 0, True, False)
                if prev:
                    if isinstance(k, int) and c == 1:
                        pe.wait_ge(s_wlo, 4 * KC)
                    pe.wait_ge(s_htlo, u)
                    at_least(pe, s_out, u - 1)
                    pe.wait_ge(s_gtc, u)
                    nc.tensor.matmul(y_ps[:, :], gt_rows[:, :], b2_rows[:, :], start=True, stop=False)
                    product(y_ps, ht_hi, ht_lo, w2_hi, w2_lo, 0, False, True).then_inc(s_y, 1)
                if cur:
                    pe.wait_ge(s_xn2, u + 1)
                    at_least(pe, s_x2lo, u)
                    transpose_rows(t2_ps, xn2[:, :]).then_inc(s_x2t, 1)
                if nx2:
                    pe.wait_ge(s_xn, v + 1)
                    at_least(pe, s_htlo, u)
                    at_least(pe, s_xtlo, v)
                    transpose_rows(t13_ps, xn[:, :]).then_inc(s_xt, 1)
                    at_least(pe, s_mtlo, v)
                    sum_item(items_to(pe, further, v), 0, True)
                    more_items(pe, v, items, c + 2, further, (), (),
                               lambda n: sum_item(n, 1, False), lambda n: trip(n, ITEMS), lambda j, n: trip(n, 0))
                if cur:
                    if isinstance(k, int) and c == 0:
                        pe.wait_ge(s_wlo, 3 * KC)
                        pe.wait_ge(s_pre, 33)
                    def route(part, start):
                        for c_ in range(KC):
                            last = nc.tensor.matmul(r_ps[0:2 * X, 0:P], wr[:, c_, :], part[:, c_, :],
                                                    start=start and c_ == 0, stop=not start and c_ == KC - 1)
                        return last

                    def hidden(part, weights, c_from, c_to):
                        for c_ in range(c_from, c_to):
                            last = nc.tensor.matmul(h_ps[:, :], part[:, c_, :], weights[:, c_, :], start=False,
                                                    stop=part is x2t_lo and c_ == KC - 1)
                        return last

                    pe.wait_ge(s_x2hi, u + 1)
                    at_least(pe, s_gtc, u)
                    route(x2t_hi, True)
                    at_least(pe, s_hg, u)
                    nc.tensor.matmul(h_ps[:, :], ones2[:, :], b1_rows[:, :], start=True, stop=False)
                    hidden(x2t_hi, w1_hi, 0, 2)
                    pe.wait_ge(s_x2lo, u + 1)
                    route(x2t_lo, False).then_inc(s_lgt, 1)
                    hidden(x2t_hi, w1_hi, 2, KC)
                    hidden(x2t_hi, w1_lo, 0, 1)
                    pe.wait_ge(s_lgc, u + 1)
                    hidden(x2t_hi, w1_lo, 1, 2)
                    nc.tensor.transpose(r_ps[:, 128:128 + 2 * X], lgt[:, :], ident[0:2 * X, 0:2 * X]).then_inc(s_lg, 1)
                    hidden(x2t_hi, w1_lo, 2, KC)
                    hidden(x2t_lo, w1_hi, 0, KC).then_inc(s_h, 1)

            pe.wait_ge(s_pre, 22)
            periods(pe, period)

        @block.vector
        def _(dve):
            def upto(n):
                dve.wait_ge(s_pre, n)

            dve.wait_ge(s_const, 17)
            dve.wait_ge(s_dst, 32)
            dve.tensor_scalar(hi_i[:, :], dst_all[:, :], 7, None, op0=ALU.arith_shift_right).then_inc(s_pre, 1)
            dve.tensor_scalar(lo_i[:, :], dst_all[:, :], P - 1, None, op0=ALU.bitwise_and).then_inc(s_pre, 1)
            dve.tensor_copy(iota16[:, :], iota_i[:, :]).then_inc(s_pre, 1)
            upto(1)
            dve.tensor_copy(dst_tile[:, :], hi_i[:, :]).then_inc(s_pre, 1)
            upto(2)
            dve.tensor_copy(dst_node[:, :], lo_i[:, :]).then_inc(s_pre, 1)
            upto(5)
            for c0, c1 in blocks:
                dve.tensor_tensor(in_tile[:, c0:c1, :], dst_tile[:, c0:c1].unsqueeze(2).broadcast_to((P, c1 - c0, TILES)),
                                  iota16[:, 0:TILES].unsqueeze(1).broadcast_to((P, c1 - c0, TILES)),
                                  op=ALU.is_equal).then_inc(s_block, 1)
                dve.tensor_tensor(in_node[:, c0:c1, :], dst_node[:, c0:c1].unsqueeze(2).broadcast_to((P, c1 - c0, P)),
                                  iota16[:, :].unsqueeze(1).broadcast_to((P, c1 - c0, P)),
                                  op=ALU.is_equal).then_inc(s_block, 1)
            dve.tensor_copy(iota[:, :], iota_i[:, :]).then_inc(s_pre, 1)
            dve.tensor_copy(deg_tab[:, P:P + 1], base_i[:, :]).then_inc(s_pre, 1)
            dve.wait_ge(s_pairs, 32)
            dve.tensor_tensor(falls[:, :], dst_a[:, :], dst_b[:, :], op=ALU.is_gt).then_inc(s_pre, 1)
            upto(8)
            dve.tensor_reduce(fall[:, :], falls[:, :], axis=AX.X, op=ALU.add).then_inc(s_pre, 1)
            dve.wait_ge(s_hist, 1)
            dve.tensor_reduce(count[:, :], r_ps[0:TILES, 0:P], axis=AX.X, op=ALU.add).then_inc(s_pre, 1)
            dve.tensor_scalar(degree[:, :], r_ps[0:TILES, 0:P], 1.0, None, op0=ALU.max).then_inc(s_pre, 1)
            upto(11)
            dve.reciprocal(deg_tab[:, 0:P], degree[:, :]).then_inc(s_pre, 1)
            dve.wait_ge(s_span, 2)
            dve.tensor_copy(span[:, :, :], m_ps[0:1, 0:2 * TILES].rearrange("p (a t) -> p a t", a=2)).then_inc(s_pre, 1)
            dve.tensor_scalar(unsorted[:, :], m_ps[0:1, 256:257], 1.0, None, op0=ALU.min).then_inc(s_pre, 1)
            upto(14)
            dve.tensor_scalar(is_sorted[:, :], unsorted[:, :], -1.0, 1.0, op0=ALU.mult, op1=ALU.add).then_inc(s_pre, 1)
            dve.tensor_scalar(items_i[:, :], span[:, 1, :], float(P - 1), None, op0=ALU.add).then_inc(s_pre, 1)
            upto(16)
            dve.tensor_scalar(items_s[:, :], items_i[:, :], 7, None, op0=ALU.arith_shift_right).then_inc(s_pre, 1)
            upto(17)
            dve.tensor_scalar(items_f[:, :], items_s[:, :], 1.0, None, op0=ALU.max).then_inc(s_pre, 1)
            upto(18)
            dve.tensor_scalar(more[:, :], items_f[:, :], -1.0, float(ALL_ITEMS), op0=ALU.mult, op1=ALU.add).then_inc(s_pre, 1)
            upto(19)
            dve.scalar_tensor_tensor(more[:, :], more[:, :], unsorted[:, 0:1], items_f[:, :],
                                     op0=ALU.mult, op1=ALU.add).then_inc(s_pre, 1)
            dve.tensor_scalar(plan[:, 0, :], span[:, 0, :], is_sorted[:, 0:1], None, op0=ALU.mult).then_inc(s_pre, 1)
            upto(20)
            dve.tensor_copy(plan[:, 1, :], more[:, :]).then_inc(s_pre, 1)
            dve.wait_ge(s_small, 16 * 7)
            dve.tensor_copy(b2_hi[:, :].bitcast(F32R), b2_stage[:, :]).then_inc(s_pre, 1)
            dve.tensor_copy(b1_hi[:, :].bitcast(F32R), b1_stage[:, :]).then_inc(s_pre, 1)
            dve.tensor_copy(wr[:, :, 0:X], wr_stage[:, :, :]).then_inc(s_pre, 1)
            upto(25)
            dve.tensor_tensor(b2_lo[:, :], b2_stage[:, :], b2_hi[:, :], op=ALU.subtract).then_inc(s_pre, 1)
            dve.tensor_tensor(b1_lo[:, :], b1_stage[:, :], b1_hi[:, :], op=ALU.subtract).then_inc(s_pre, 1)
            dve.tensor_tensor(wr[:, :, X:2 * X], wr_stage[:, :, :], f32(wr[:, :, 0:X]), op=ALU.subtract).then_inc(s_pre, 1)
            dve.tensor_scalar(b2_hi[:, :], b2_hi[:, :], is_hi[:, 0:1], None, op0=ALU.mult).then_inc(s_pre, 1)
            dve.tensor_scalar(b1_hi[:, :], b1_hi[:, :], is_hi[0:2, 1:2], None, op0=ALU.mult).then_inc(s_pre, 1)
            upto(30)
            dve.scalar_tensor_tensor(b2_rows[:, :], b2_lo[:, :], is_lo[:, 0:1], b2_hi[:, :], op0=ALU.mult, op1=ALU.add).then_inc(s_pre, 1)
            dve.scalar_tensor_tensor(b1_rows[:, :], b1_lo[:, :], is_lo[0:2, 1:2], b1_hi[:, :], op0=ALU.mult, op1=ALU.add).then_inc(s_pre, 1)
            dve.tensor_copy(ones2[:, :], ones[0:2, :]).then_inc(s_pre, 1)
            dve.memset(weight[:, 0:1], 1.0 / MSG_SCALE).then_inc(s_pre, 1)
            upto(34)

            further = dve.alloc_register("dve_further")
            seconds = dve.alloc_register("dve_seconds")
            laters = dve.alloc_register("dve_laters")
            dve.reg_mov(further, 0)
            dve.reg_mov(seconds, 0)
            dve.reg_mov(laters, 0)

            def trips_to(v):
                return 0 if isinstance(v, int) and v == 0 else dve.snap(seconds) + dve.snap(laters) + v

            def edge_stats(t, slot, edges, loaded, loads, rd, gathers):
                dve.wait_ge(loaded, loads)
                dve.tensor_scalar(rel[:, :], edges[:, :, 1], rdeg[:, rd, P:P + 1], None,
                                  op0=ALU.subtract).then_inc(s_es, 1)
                for a in range(ITEMS):
                    dve.wait_ge(s_raw[slot][a], gathers)
                    dve.bn_stats(stat_e[:, a, :], raw[:, slot, a, :]).then_inc(s_es, 1)

            def edge_weights(t, n, rows, rd):
                base = t * EDGE_STEPS
                dve.wait_ge(s_es, base + 1)
                if rows == 0:
                    at_least(dve, s_sum, n)
                for a in range(ITEMS):
                    dve.tensor_scalar(onehot[:, rows + a, :], iota[:, :], rel[:, a:a + 1], None, op0=ALU.is_equal).then_inc(s_es, 1)
                for a in range(ITEMS):
                    wait_apart(dve, (s_es, base + 2 + a))
                    dve.bn_aggr(mv[:, 1 + a, :], stat_e[:, a, :]).then_inc(s_es, 1)
                for a in range(ITEMS):
                    dve.wait_ge(s_es, base + 4 + a)
                    dve.scalar_tensor_tensor(weighted[:, a, :], onehot[:, rows + a, :], 1.0, rdeg[:, rd, 0:P], op0=ALU.mult,
                                             op1=ALU.mult, accum_out=weight[:, 1 + a:2 + a]).then_inc(s_es, 1)

            def edge_scale_step(i, t, n, lanes):
                if i == 0:
                    dve.wait_ge(s_guess, t + 1)
                    dve.scalar_tensor_tensor(newton[:, lanes], guess[:, lanes], -0.5, guess[:, lanes],
                                             op0=ALU.mult, op1=ALU.mult).then_inc(s_es, 1)
                    return
                dve.wait_ge(s_es, t * EDGE_STEPS + 9 + i)
                if i == 1:
                    dve.scalar_tensor_tensor(newton[:, lanes], mv[:, lanes, 1], EPS, newton[:, lanes],
                                             op0=ALU.add, op1=ALU.mult).then_inc(s_es, 1)
                elif i == 2:
                    dve.scalar_tensor_tensor(rstd[:, lanes], newton[:, lanes], 1.5, guess[:, lanes],
                                             op0=ALU.add, op1=ALU.mult).then_inc(s_es, 1)
                elif i == 3:
                    at_least(dve, s_mhi, n)
                    dve.scalar_tensor_tensor(scale[:, lanes], rstd[:, lanes], MSG_SCALE, weight[:, lanes],
                                             op0=ALU.mult, op1=ALU.mult).then_inc(s_es, 1)
                else:
                    dve.scalar_tensor_tensor(shift[:, lanes], mv[:, lanes, 0], -1.0, scale[:, lanes],
                                             op0=ALU.mult, op1=ALU.mult).then_inc(s_es, 1)

            def period(k, c):
                prev, cur, nx1, nx2, nx3, nx4 = known(k, c)
                u = tile_of(k, c)
                v = u + 2

                def norm2(n):
                    if not cur:
                        return
                    base = NORM2_STEPS * u
                    if n == 0:
                        dve.wait_ge(s_z, u + 1)
                        dve.scalar_tensor_tensor(x1[:, c % 2, :], z_ps[c % 2][:, :], 0.0, x_in[:, c % 4, :],
                                                 op0=ALU.max, op1=ALU.add).then_inc(s_x1, 1)
                    elif n == 1:
                        dve.wait_ge(s_x1, u + 1)
                        dve.bn_stats(stat2[:, :], x1[:, c % 2, :]).then_inc(s_n2, 1)
                    elif n == 2:
                        wait_apart(dve, (s_n2, base + 1))
                        dve.bn_aggr(mv2[:, :], stat2[:, :]).then_inc(s_n2, 1)
                    elif n == 3:
                        dve.wait_ge(s_n2, base + 2)
                        dve.wait_ge(s_guess2, u + 1)
                        dve.scalar_tensor_tensor(newton2[:, :], guess2[:, :], -0.5, guess2[:, :],
                                                 op0=ALU.mult, op1=ALU.mult).then_inc(s_n2, 1)
                    elif n == 4:
                        dve.wait_ge(s_n2, base + 3)
                        dve.scalar_tensor_tensor(newton2[:, :], mv2[:, 1:2], EPS, newton2[:, :],
                                                 op0=ALU.add, op1=ALU.mult).then_inc(s_n2, 1)
                    elif n == 5:
                        dve.wait_ge(s_n2, base + 4)
                        at_least(dve, s_xn2, u)
                        dve.scalar_tensor_tensor(rstd2[:, :], newton2[:, :], 1.5, guess2[:, :],
                                                 op0=ALU.add, op1=ALU.mult).then_inc(s_n2, 1)
                    elif n == 6:
                        dve.wait_ge(s_n2, base + 5)
                        dve.scalar_tensor_tensor(shift2[:, :], mv2[:, 0:1], -1.0, rstd2[:, :],
                                                 op0=ALU.mult, op1=ALU.mult).then_inc(s_n2, 1)

                def hidden_lo():
                    if prev:
                        dve.wait_ge(s_hthi, u)
                        at_least(dve, s_y, u - 1)
                        dve.tensor_tensor(ht_lo[:, :, :], t13_ps[:, :].rearrange("p (c n) -> p c n", c=KC),
                                          f32(ht_hi[:, :, :]), op=ALU.subtract).then_inc(s_htlo, 1)

                if prev:
                    dve.wait_ge(s_h, u)
                    at_least(dve, s_ht, u - 1)
                    dve.scalar_tensor_tensor(hid[:, :, :], h_ps[:, :].rearrange("p (x f) -> p x f", x=X), 0.0,
                                             gate[:, :].unsqueeze(2).broadcast_to((P, X, F)),
                                             op0=ALU.max, op1=ALU.mult).then_inc(s_hg, 1)
                if nx2:
                    items = dve.value_load(plan[0:1, 1, bass.ds(v, 1)], min_val=1, max_val=ALL_ITEMS)
                if nx1:
                    dve.wait_ge(s_mthi, u + 2)
                    at_least(dve, s_z, u)
                    dve.scalar_tensor_tensor(mt_lo[:, (c + 1) % 2, :, :], m_ps[:, :].rearrange("p (c n) -> p c n", c=KC),
                                             1.0 / MSG_SCALE, f32(mt_hi[:, (c + 1) % 2, :, :]), op0=ALU.mult,
                                             op1=ALU.subtract).then_inc(s_mtlo, 1)
                norm2(0)
                hidden_lo()
                for i in range(1, 7):
                    norm2(i)
                if nx2:
                    def second_trip(n):
                        t, gathers = trips_to(v + 1), dve.snap(seconds) * 16 + 16
                        edge_stats(t, 2, edge_further[:, 0, :, :], s_further[0],
                                   gathers, (c + 2) % 4, gathers)
                        edge_weights(t, n, ITEMS, (c + 2) % 4)
                        for i in range(5):
                            edge_scale_step(i, t, n, slice(1, LANES))

                    def later_trip(j, n):
                        t, loads = trips_to(v + 1), dve.snap(laters) * 16 + 16
                        edge_stats(t, 3, edge_further[:, 1, :, :], s_further[1], loads, (c + 2) % 4, loads)
                        edge_weights(t, n, 0, (c + 2) % 4)
                        for i in range(5):
                            edge_scale_step(i, t, n, slice(1, LANES))

                    more_items(dve, v, items, c + 2, further, (seconds,), (laters,), None, second_trip, later_trip)
                if nx3:
                    w = v + 1
                    t = trips_to(w)
                    dve.wait_ge(s_rdeg[(c + 3) % 4], 16 * (uses(k, c + 3, 4) + 1))
                    edge_stats(t, (c + 3) % 2, edge[:, (c + 3) % 4, :, :], s_edge[(c + 3) % 4],
                               16 * (uses(k, c + 3, 4) + 1), (c + 3) % 4, 16 * (uses(k, c + 3, 2) + 1))
                    dve.wait_ge(s_x[(c + 3) % 4], 16 * (uses(k, c + 3, 4) + 1))
                    dve.bn_stats(stat[:, :], x_in[:, (c + 3) % 4, :]).then_inc(s_norm, 1)
                if prev:
                    dve.wait_ge(s_y, u)
                    at_least(dve, s_st[(c - 1) % 2], 16 * uses(k, c - 1, 2))
                    dve.tensor_tensor(o_sb[:, (c - 1) % 2, :], y_ps[:, :], x1[:, (c - 1) % 2, :],
                                      op=ALU.add).then_inc(s_out, 1)
                if cur:
                    dve.wait_ge(s_x2hi, u + 1)
                    at_least(dve, s_h, u)
                    dve.tensor_tensor(x2t_lo[:, :, :], t2_ps[:, :].rearrange("p (c n) -> p c n", c=KC),
                                      f32(x2t_hi[:, :, :]), op=ALU.subtract).then_inc(s_x2lo, 1)
                if nx2:
                    dve.wait_ge(s_xthi, v + 1)
                    dve.tensor_tensor(xt_lo[:, :, :], t13_ps[:, :].rearrange("p (c n) -> p c n", c=KC),
                                      f32(xt_hi[:, :, :]), op=ALU.subtract).then_inc(s_xtlo, 1)
                if nx3:
                    n = items_to(dve, further, w)
                    t = trips_to(w)

                    wait_apart(dve, (s_norm, NORM_STEPS * w + 1))
                    dve.bn_aggr(mv[:, 0, :], stat[:, :]).then_inc(s_norm, 1)
                    edge_weights(t, n, 0, (c + 3) % 4)

                def scale_step(i):
                    if nx3:
                        edge_scale_step(i, t, n, slice(0, LANES))

                if cur:
                    def routed(n):
                        dve.wait_ge(s_rt, ROUTE_STEPS * u + n)

                    dve.wait_ge(s_lg, u + 1)
                    at_least(dve, s_gt, u)
                    dve.tensor_reduce(lg[:, :], r_ps[:, 128:128 + 2 * X].rearrange("p (a x) -> p x a", a=2),
                                      axis=AX.X, op=ALU.add).then_inc(s_rt, 1)
                scale_step(0)
                if cur:
                    routed(1)
                    dve.tensor_reduce(neg_max[:, :], lg[:, :], axis=AX.X, op=ALU.max, negate=True).then_inc(s_rt, 1)
                    dve.tensor_tensor(lg_diff[:, :, :], lg[:, :].unsqueeze(1).broadcast_to((P, X, X)),
                                      lg[:, :].unsqueeze(2).broadcast_to((P, X, X)), op=ALU.subtract).then_inc(s_rt, 1)
                scale_step(1)
                if cur:
                    routed(3)
                    dve.tensor_tensor(beats[:, :, :], lg_diff[:, :, :], tie_bar[:, :, :], op=ALU.is_ge).then_inc(s_rt, 1)
                scale_step(2)
                if cur:
                    routed(4)
                    dve.tensor_reduce(rank[:, :], beats[:, :, :], axis=AX.X, op=ALU.add).then_inc(s_rt, 1)
                scale_step(3)
                if cur:
                    dve.wait_ge(s_exp, u + 1)
                    dve.reciprocal(r_sum[:, :], ex_sum[:, :]).then_inc(s_rt, 1)
                scale_step(4)
                if cur:
                    routed(6)
                    dve.scalar_tensor_tensor(ex_top[:, :], rank[:, :], 1.5, ex[:, :], op0=ALU.is_lt, op1=ALU.mult).then_inc(s_rt, 1)
                    routed(7)
                    dve.tensor_scalar(gate[:, :], ex_top[:, :], r_sum[:, 0:1], None, op0=ALU.mult).then_inc(s_rt, 1)
                    dve.tensor_scalar(gate_parts[:, 0:2, :].bitcast(F32R), ex_top[:, :].unsqueeze(1).broadcast_to((P, 2, X)),
                                      r_sum[:, 0:1], None, op0=ALU.mult).then_inc(s_rt, 1)
                    routed(9)
                    dve.tensor_tensor(gate_parts[:, 2, :], gate[:, :], gate_parts[:, 0, :], op=ALU.subtract).then_inc(s_rt, 1)

            periods(dve, period)

    return nc


_OUT = ((10000, 512), "float32")


def kernel(x, src, dst, L0_gnn_w, L0_ffn_Wr, L0_ffn_br, L0_ffn_W1, L0_ffn_b1, L0_ffn_W2, L0_ffn_b2):
    import numpy as np
    import concourse.bacc as bacc
    from concourse.bass_utils import run_bass_kernel_spmd

    w1 = np.asarray(L0_ffn_W1)
    w2 = np.asarray(L0_ffn_W2)
    X, D, F = w1.shape
    arrays = {
        "x": np.asarray(x),
        "edges": np.stack([np.asarray(src), np.asarray(dst)], axis=1),
        "dst": np.asarray(dst),
        "w_gnn": np.asarray(L0_gnn_w).T,
        "w_router": np.asarray(L0_ffn_Wr),
        "b_router": np.asarray(L0_ffn_br),
        "w1": w1.transpose(1, 0, 2).reshape(D, X * F),
        "b1": np.asarray(L0_ffn_b1).reshape(X * F),
        "w2": w2.reshape(X * F, D),
        "b2": np.asarray(L0_ffn_b2),
    }
    nc = bacc.Bacc("TRN2", target_bir_lowering=False, num_devices=1)
    feed, args = {}, []
    for name, a in arrays.items():
        a = np.ascontiguousarray(a)
        feed[f"in_{name}"] = a
        args.append(nc.dram_tensor(f"in_{name}", a.shape, mybir.dt.from_np(a.dtype), kind="ExternalInput").ap())
    shape, dtype = _OUT
    args.append(nc.dram_tensor("out_0", shape, mybir.dt.from_np(np.dtype(dtype)), kind="ExternalOutput").ap())
    moe_gnn_kernel(nc, *args)
    r = run_bass_kernel_spmd(nc, [feed], core_ids=[0])
    return r.results[0]["out_0"]
```
